# Optimizing a Trainium2 kernel written in Bass

```python
import numpy as np
import jax
import jax.numpy as jnp

def _softmax(x, axis=-1):
    return jax.nn.softmax(x, axis=axis)

def _gelu(x):
    return jax.nn.gelu(x, approximate=True)

def _silu(x):
    return jax.nn.silu(x)

def _sigmoid(x):
    return jax.nn.sigmoid(x)

def _layernorm(x, axis=-1, eps=1e-05):
    m = jnp.mean(x, axis=axis, keepdims=True)
    v = jnp.var(x, axis=axis, keepdims=True)
    return (x - m) / jnp.sqrt(v + eps)

def _scatter_add(tgt, idx, src, axis=0):
    return tgt.at[idx].add(src)

def _segment_sum(src, seg, n):
    return jax.ops.segment_sum(src, seg, n)
kernel_name = 'mk_seq_preln_d1_jaxref_r8_cb44a8'

def setup_inputs(seed: int=0):
    np.random.seed(seed)
    _w = jnp.asarray

    def _L0_attn_setup():
        import jax, jax.numpy as jnp
        import numpy as np
        FEATS = 128
        HEAD = 16
        HEAD_DIM = FEATS // HEAD
        EPS = 1e-12

        def _l2norm(t):
            n = jnp.sqrt(jnp.sum(t * t, axis=-1, keepdims=True))
            return t / jnp.maximum(n, EPS)
        key = jax.random.key(seed)
        ks = jax.random.split(key, 10)
        s = 0.02
        inp = {'x': jax.random.normal(ks[0], (4, 256, FEATS), dtype=jnp.float32), 'Wq': jax.random.normal(ks[1], (FEATS, FEATS), dtype=jnp.float32) * s, 'bq': jnp.zeros((FEATS,), dtype=jnp.float32), 'Wk': jax.random.normal(ks[2], (FEATS, FEATS), dtype=jnp.float32) * s, 'bk': jnp.zeros((FEATS,), dtype=jnp.float32), 'Wv': jax.random.normal(ks[3], (FEATS, FEATS), dtype=jnp.float32) * s, 'bv': jnp.zeros((FEATS,), dtype=jnp.float32), 'Wo': jax.random.normal(ks[4], (FEATS, FEATS), dtype=jnp.float32) * s, 'bo': jnp.zeros((FEATS,), dtype=jnp.float32), 'm': jnp.full((HEAD,), 0.5, dtype=jnp.float32)}
        return inp
    _L0_attn_in = _L0_attn_setup()

    def _L0_ffn_setup():
        import jax, jax.numpy as jnp
        import numpy as np
        B, S, H = (2, 256, 128)
        N, F, SF, K = (16, 128, 512, 1)
        key = jax.random.key(seed)
        ks = jax.random.split(key, 7)
        std = 0.02
        return {'hidden_states': jax.random.normal(ks[0], (B, S, H), dtype=jnp.float32), 'router_w': jax.random.normal(ks[1], (N, H), dtype=jnp.float32) * std, 'gate_up_proj': jax.random.normal(ks[2], (N, H, 2 * F), dtype=jnp.float32) * std, 'down_proj': jax.random.normal(ks[3], (N, F, H), dtype=jnp.float32) * std, 'shared_gate_w': jax.random.normal(ks[4], (SF, H), dtype=jnp.float32) * std, 'shared_up_w': jax.random.normal(ks[5], (SF, H), dtype=jnp.float32) * std, 'shared_down_w': jax.random.normal(ks[6], (H, SF), dtype=jnp.float32) * std}
    _L0_ffn_in = _L0_ffn_setup()
    _d = {'L0_attn_x': _L0_attn_in['x'], 'L0_attn_Wq': _L0_attn_in['Wq'], 'L0_attn_bq': _L0_attn_in['bq'], 'L0_attn_Wk': _L0_attn_in['Wk'], 'L0_attn_bk': _L0_attn_in['bk'], 'L0_attn_Wv': _L0_attn_in['Wv'], 'L0_attn_bv': _L0_attn_in['bv'], 'L0_attn_Wo': _L0_attn_in['Wo'], 'L0_attn_bo': _L0_attn_in['bo'], 'L0_attn_m': _L0_attn_in['m'], 'L0_ffn_router_w': _L0_ffn_in['router_w'], 'L0_ffn_gate_up_proj': _L0_ffn_in['gate_up_proj'], 'L0_ffn_down_proj': _L0_ffn_in['down_proj'], 'L0_ffn_shared_gate_w': _L0_ffn_in['shared_gate_w'], 'L0_ffn_shared_up_w': _L0_ffn_in['shared_up_w'], 'L0_ffn_shared_down_w': _L0_ffn_in['shared_down_w']}
    _x0 = _d['L0_attn_x']
    _d['L0_attn_x'] = jax.random.normal(jax.random.fold_in(jax.random.key(seed), 1), (4, 1024, 128), dtype=_x0.dtype)
    del _x0
    return _d

def reference(L0_attn_x, L0_attn_Wq, L0_attn_bq, L0_attn_Wk, L0_attn_bk, L0_attn_Wv, L0_attn_bv, L0_attn_Wo, L0_attn_bo, L0_attn_m, L0_ffn_router_w, L0_ffn_gate_up_proj, L0_ffn_down_proj, L0_ffn_shared_gate_w, L0_ffn_shared_up_w, L0_ffn_shared_down_w):

    def _L0_attn_ref(x, Wq, bq, Wk, bk, Wv, bv, Wo, bo, m):
        import jax, jax.numpy as jnp
        import numpy as np
        FEATS = 128
        HEAD = 16
        HEAD_DIM = FEATS // HEAD
        EPS = 1e-12

        def _l2norm(t):
            n = jnp.sqrt(jnp.sum(t * t, axis=-1, keepdims=True))
            return t / jnp.maximum(n, EPS)
        b, n, f = x.shape

        def proj(W, bias):
            y = x @ W + bias
            return y.reshape(b, n, HEAD, HEAD_DIM).transpose(0, 2, 1, 3)
        q = _l2norm(proj(Wq, bq))
        k = _l2norm(proj(Wk, bk))
        v = proj(Wv, bv)
        sim = jnp.einsum('bhid,bhjd->bhij', q, k)
        sigma_m = jax.nn.sigmoid(m).reshape(1, HEAD, 1, 1)
        scaling = jnp.asarray(n, dtype=x.dtype) ** sigma_m
        attn = sim / scaling
        out = jnp.einsum('bhij,bhjd->bhid', attn, v)
        out = out.transpose(0, 2, 1, 3).reshape(b, n, f)
        return out @ Wo + bo

    def _L0_ffn_ref(hidden_states, router_w, gate_up_proj, down_proj, shared_gate_w, shared_up_w, shared_down_w):
        import jax, jax.numpy as jnp
        import numpy as np
        B, S, H = (2, 256, 128)
        N, F, SF, K = (16, 128, 512, 1)
        b, s, h = hidden_states.shape
        hidden = hidden_states.reshape(-1, h)
        t = hidden.shape[0]
        logits = hidden @ router_w.T
        top_vals, top_idx = jax.lax.top_k(logits, K)
        scores = jnp.full_like(logits, -jnp.inf)
        scores = scores.at[jnp.arange(t)[:, None], top_idx].set(top_vals)
        scores = jax.nn.sigmoid(scores.astype(jnp.float32)).astype(hidden.dtype)
        routed_in = hidden[None, :, :] * scores.T[:, :, None]
        gate_up = jnp.einsum('nth,nhf->ntf', routed_in, gate_up_proj)
        gate, up = jnp.split(gate_up, 2, axis=-1)
        routed_out = jnp.einsum('ntf,nfh->nth', up * jax.nn.silu(gate), down_proj)
        expert_sum = routed_out.sum(axis=0)
        shared = jax.nn.silu(hidden @ shared_gate_w.T) * (hidden @ shared_up_w.T) @ shared_down_w.T
        return (shared + expert_sum).reshape(b, s, h)
    x = L0_attn_x
    x = x + _L0_attn_ref(_layernorm(x, axis=-1), L0_attn_Wq, L0_attn_bq, L0_attn_Wk, L0_attn_bk, L0_attn_Wv, L0_attn_bv, L0_attn_Wo, L0_attn_bo, L0_attn_m)
    x = x + _L0_ffn_ref(_layernorm(x, axis=-1), L0_ffn_router_w, L0_ffn_gate_up_proj, L0_ffn_down_proj, L0_ffn_shared_gate_w, L0_ffn_shared_up_w, L0_ffn_shared_down_w)
    return x

_drawn_inputs = setup_inputs


def setup_inputs(seed=0):
    import zlib

    import numpy as np

    out = dict(_drawn_inputs(seed))
    spreads = {'L0_attn_bq': (0.0, 0.392),
     'L0_attn_bk': (0.0, 0.1),
     'L0_attn_bv': (0.0, 0.1),
     'L0_attn_bo': (0.0, 0.1),
     'L0_attn_m': (0.5, 0.6)}
    factors = {'L0_ffn_router_w': 8.0,
     'L0_ffn_gate_up_proj': 8.0,
     'L0_ffn_down_proj': 8.0,
     'L0_ffn_shared_gate_w': 4.85,
     'L0_ffn_shared_up_w': 4.812,
     'L0_ffn_shared_down_w': 4.825}
    for name, (base, spread) in spreads.items():
        noise = np.random.default_rng([zlib.crc32(name.encode()), seed]).standard_normal(out[name].shape)
        drawn = base * np.exp(spread * noise) if base else spread * noise
        out[name] = jnp.asarray(drawn.astype(out[name].dtype))
    for name, factor in factors.items():
        out[name] = (out[name] * factor).astype(out[name].dtype)
    return out
```

```python
from contextlib import ExitStack

import numpy as np

import concourse.bass as bass
from concourse import mybir

ALU = mybir.AluOpType
ACT = mybir.ActivationFunctionType
AX = mybir.AxisListType
F32 = mybir.dt.float32
I32 = mybir.dt.int32

P = 128


def build_block(nc, x, Wq, bq, Wk, bk, Wv, bv, Wo, bo, m, router_w, gate_up, down, shared_gate, shared_up,
                shared_down, out):
    B, S, D = x.shape
    HEADS = m.shape[0]
    HD = D // HEADS
    E, _, F2 = gate_up.shape
    F = F2 // 2
    SF = shared_gate.shape[0]
    T = B * S
    NT = T // P
    TB = S // P
    Q = 4
    NQ = NT // Q
    QB = TB // Q
    KC = SF // P
    NG = -(-(NT + E - 1) // Q)
    SLOT_TILES = NG * Q
    SLOTS = SLOT_TILES * P
    QKV = 3 * D
    WE = F2 + D
    EPS = 1e-5
    C1 = 5
    assert D == P and F == P and QB == 2 and NG == 12 and KC == 4

    x_slots = nc.dram_tensor("x_slots", (SLOTS, D), F32, kind="Internal").ap()
    y_slots = nc.dram_tensor("y_slots", (SLOTS, D), F32, kind="Internal").ap()
    x_rows = x.rearrange("b (j p) d -> p (b j) d", p=P)
    out_rows = out.rearrange("b (j p) d -> p (b j) d", p=P)

    with ExitStack() as ctx:
        def sb(name, shape, dt=F32):
            return ctx.enter_context(nc.sbuf_tensor(name, shape, dt))

        def sem(name):
            return ctx.enter_context(nc.semaphore(name))

        xres = sb("xres", [P, NT, D])
        xn = sb("xn", [P, NT, D])
        hT = sb("hT", [P, T])
        gath = sb("gath", [P, NT, D])
        qkv = sb("qkv", [P, 2, TB, QKV])
        sq = sb("sq", [P, 2, Q, 2 * D])
        xnT = sb("xnT", [P, 2, Q * P])
        qT = sb("qT", [P, 2, Q * P])
        st1 = sb("st1", [P, NT, 6])
        mv1 = sb("mv1", [P, NT, 2])
        rs1 = sb("rs1", [P, NT])
        st2 = sb("st2", [P, NT, 6])
        mv2 = sb("mv2", [P, NT, 2])
        rs2 = sb("rs2", [P, NT])
        ss = sb("ss", [P, 2, TB, 2 * HEADS])
        rn = sb("rn", [P, 2, TB, 2 * HEADS])
        vkm = sb("vkm", [P, 2, D])
        wb = sb("wb", [P, 2, D])
        w_qkv = sb("w_qkv", [P, QKV])
        b_qkv = sb("b_qkv", [P, QKV])
        w_o = sb("w_o", [P, D])
        b_o = sb("b_o", [P, D])
        m_col = sb("m_col", [P, 1])
        m_tmp = sb("m_tmp", [P, 4])
        head_mask = sb("head_mask", [P, D])
        ident = sb("ident", [P, P])
        before = sb("before", [P, P])
        ones = sb("ones", [P, P])
        eps_col = sb("eps_col", [P, 1])
        zero_col = sb("zero_col", [P, 1])
        rw_in = sb("rw_in", [E, D])
        rwT = sb("rwT", [P, E])
        sg_in = sb("sg_in", [P, KC, D])
        su_in = sb("su_in", [P, KC, D])
        sd_in = sb("sd_in", [P, SF])
        sgT = sb("sgT", [P, SF])
        suT = sb("suT", [P, SF])
        sdT = sb("sdT", [P, KC, D])
        w_e = sb("w_e", [P, E, WE])
        rank_key = sb("rank_key", [P, NT, E])
        run_mask = sb("run_mask", [P, E, NT])
        top = sb("top", [P, NT])
        score = sb("score", [P, NT])
        key = sb("key", [P, NT, E])
        ktop = sb("ktop", [P, NT])
        hot = sb("hot", [P, E, NT])
        run = sb("run", [P, E, NT])
        cnt = sb("cnt", [P, E])
        tot = sb("tot", [P, E])
        tot_i = sb("tot_i", [P, E], I32)
        til_i = sb("til_i", [P, E], I32)
        til = sb("til", [P, E])
        til_end = sb("til_end", [P, E])
        base = sb("base", [P, E])
        pos_f = sb("pos_f", [P, NT])
        pos = sb("pos", [P, NT], I32)
        tile_no = sb("tile_no", [1, SLOT_TILES, E])
        past = sb("past", [1, SLOT_TILES, E])
        eid_f = sb("eid_f", [1, SLOT_TILES])
        eid = sb("eid", [1, SLOT_TILES], I32)
        sg_act = sb("sg_act", [P, 2, 512])
        s_act = sb("s_act", [P, 2, 512])
        yT = sb("yT", [P, 512])
        xg = sb("xg", [P, 2, Q, D])
        xgT = sb("xgT", [P, 2, Q * P])
        eg_act = sb("eg_act", [P, 2, Q, F])
        e_act = sb("e_act", [P, 2, Q, F])
        e_actT = sb("e_actT", [P, 2, Q * P])
        yg = sb("yg", [P, 2, Q, D])

        bank = [ctx.enter_context(nc.psum_tensor(f"bank{i}", [P, 512], F32)) for i in range(4)]
        pair = ctx.enter_context(nc.psum_tensor("quad_banks", [P, 4, 512], F32))
        ps_xT, ps_qy, ps_vk, ps_log = bank
        ps_yT, ps_y = bank[0], bank[1]
        ps_gT, ps_aT, ps_yg = bank[0], bank[1], bank[2]
        setup_bank = bank[3]

        ld_x0, ld_x, ld_wa, ld_ws, ld_we = sem("ld_x0"), sem("ld_x"), sem("ld_wa"), sem("ld_ws"), sem("ld_we")
        k_id, k_pool = sem("k_id"), sem("k_pool")
        z_done, zero_st = sem("z_done"), sem("zero_st")
        dch = sem("dch")
        ach = sem("ach")
        m_step = sem("m_step")
        var1, std1, rstd1, xn_rdy, xb_rdy = sem("var1"), sem("std1"), sem("rstd1"), sem("xn_rdy"), sem("xb_rdy")
        xT_mm, xT_sb = sem("xT_mm"), sem("xT_sb")
        qkv_mm, qkv_sb, sq_done, ss_done = sem("qkv_mm"), sem("qkv_sb"), sem("sq_done"), sem("ss_done")
        ssum, nrm, rn_rdy = sem("ssum"), sem("nrm"), sem("rn_rdy")
        v_rdy, q_rdy = sem("v_rdy"), sem("q_rdy")
        vk_mm, vkm_rdy, wb_mm, wb_rdy = sem("vk_mm"), sem("vkm_rdy"), sem("wb_mm"), sem("wb_rdy")
        qT_mm, qT_sb, y_mm, x1_rdy = sem("qT_mm"), sem("qT_sb"), sem("y_mm"), sem("x1_rdy")
        var2, std2, rstd2, h_rdy = sem("var2"), sem("std2"), sem("rstd2"), sem("h_rdy")
        su_mm, su_cp, log_mm = sem("su_mm"), sem("su_cp"), sem("log_mm")
        top_rdy, score_rdy, hs_rdy, cnt_rdy, cnt_mm, pos_rdy, eid_rdy = (
            sem("top_rdy"), sem("score_rdy"), sem("hs_rdy"), sem("cnt_rdy"), sem("cnt_mm"), sem("pos_rdy"),
            sem("eid_rdy"))
        scat = sem("scat")
        s_gu_mm, s_silu, s_act_rdy, s_dn_mm, s_dn_end = (
            sem("s_gu_mm"), sem("s_silu"), sem("s_act_rdy"), sem("s_dn_mm"), sem("s_dn_end"))
        yT_sb, yT_mm, y_free = sem("yT_sb"), sem("yT_mm"), sem("y_free")
        xg_ld = [sem("xg_ld0"), sem("xg_ld1")]
        gT_mm, gT_sb, e_gu_mm, e_silu, e_act_rdy = (
            sem("gT_mm"), sem("gT_sb"), sem("e_gu_mm"), sem("e_silu"), sem("e_act_rdy"))
        aT_mm, aT_sb, e_dn_mm, yg_rdy = sem("aT_mm"), sem("aT_sb"), sem("e_dn_mm"), sem("yg_rdy")
        yg_st = [sem("yg_st0"), sem("yg_st1")]
        gat = [sem(f"gat{c}") for c in range(NQ)]
        fin, out_st = sem("fin"), sem("out_st")

        block = ctx.enter_context(nc.Block())

        def tiles(c):
            return range(Q * c, Q * c + Q)

        def gate_up_banks(par):
            return pair[:, 2 * par:2 * par + 2, :].rearrange("p a (b n) -> p (a b) n", b=2)

        def over_groups(step, eng):
            step(0, 0, (0,))
            step(0, 1, (1, 0))
            step(1, 0, (2, 1, 0))
            step(1, 1)
            step(2, 0)
            step(2, 1)
            with eng.Fori(3, NG // 2) as i:
                step(i, 0)
                step(i, 1)
            step(NG // 2, 0, (3, 2, 1))
            step(NG // 2, 1, (3, 2))
            step(NG // 2 + 1, 0, (3,))

        @block.sync
        def _(sp):
            sp.dma_start(xres[:, 0:TB, :], x_rows[:, 0:TB, :]).then_inc(ld_x0, 16)
            for b in range(1, B):
                sp.dma_start(xres[:, b * TB:(b + 1) * TB, :], x_rows[:, b * TB:(b + 1) * TB, :]).then_inc(ld_x, 16)
            sp.dma_start(sg_in[:], shared_gate.rearrange("(k f) h -> f k h", f=P)).then_inc(ld_ws, 16)
            sp.dma_start(su_in[:], shared_up.rearrange("(k f) h -> f k h", f=P)).then_inc(ld_ws, 16)
            sp.dma_start(sd_in[:], shared_down).then_inc(ld_ws, 16)
            sp.dma_start(rw_in[:], router_w).then_inc(ld_ws, 16)
            sp.wait_ge(z_done, 1)
            rows = x_slots.rearrange("(p r) d -> p (r d)", p=P)
            zeros = gath[:, 0:SLOT_TILES // 4, :].rearrange("p j d -> p (j d)")
            for i in range(4):
                sp.dma_start(rows[:, i * zeros.shape[1]:(i + 1) * zeros.shape[1]], zeros).then_inc(zero_st, 16)
            sp.dma_start(w_e[:, :, 0:F2], gate_up.rearrange("e h f -> h e f")).then_inc(ld_we, 16)
            sp.dma_start(w_e[:, :, F2:WE], down.rearrange("e f h -> f e h")).then_inc(ld_we, 16)

            def slots(dram, g):
                return dram[bass.ds(g * (Q * P), Q * P), :].rearrange("(j p) d -> p j d", p=P)

            def load_group(g, par):
                sp.dma_start(xg[:, par], slots(x_slots, g)).then_inc(xg_ld[par], 16)

            def experts(i, par, stages=(3, 2, 1, 0)):
                g = i * 2 + par
                if 3 in stages:
                    sp.wait_ge(yg_rdy, g - 2)
                    sp.dma_start(slots(y_slots, g - 3), yg[:, (par - 3) % 2]).then_inc(yg_st[(par - 3) % 2], 16)
                if 0 in stages:
                    if not (isinstance(i, int) and g < 2):
                        sp.wait_ge(gT_mm, g - 1)
                    load_group(g, par)

            sp.wait_ge(scat, 16 * NT)
            over_groups(experts, sp)
            for c in range(NQ):
                sp.wait_ge(fin, c + 1)
                sp.dma_start(out_rows[:, Q * c:Q * c + Q, :], gath[:, Q * c:Q * c + Q, :]).then_inc(out_st, 16)
            sp.wait_ge(out_st, 16 * NQ)

        @block.gpsimd
        def _(pool):
            g = nc.gpsimd
            g.memset(ident[:], 0.0)
            g.memset(before[:], 1.0)
            g.memset(ones[:], 1.0)
            g.memset(head_mask[:], 1.0)
            g.memset(run_mask[:], 1.0)
            g.memset(eps_col[:], EPS)
            g.memset(zero_col[:], 0.0)
            g.memset(gath[:, 0:SLOT_TILES // 4, :], 0.0).then_inc(z_done, 1)
            pool.wait_ge(z_done, 1)
            g.affine_select(out=ident[:], in_=ident[:], compare_op=ALU.not_equal, fill=1.0, base=0,
                            pattern=[[-1, P]], channel_multiplier=1).then_inc(k_id, 1)
            g.affine_select(out=before[:], in_=before[:], compare_op=ALU.is_gt, fill=0.0, base=0,
                            pattern=[[1, P]], channel_multiplier=-1)
            g.affine_select(out=head_mask[:], in_=head_mask[:], compare_op=ALU.is_ge, fill=0.0, base=0,
                            pattern=[[-HD, HEADS], [0, HD]], channel_multiplier=1).then_inc(k_pool, 1)
            g.affine_select(out=run_mask[:], in_=run_mask[:], compare_op=ALU.not_equal, fill=0.0, base=0,
                            pattern=[[0, E], [1, NT]], channel_multiplier=0)
            g.iota(rank_key[:], pattern=[[0, NT], [-1, E]], base=E, channel_multiplier=0,
                   allow_small_or_imprecise_dtypes=True)
            g.iota(tile_no[:], pattern=[[1, SLOT_TILES], [0, E]], base=0, channel_multiplier=0,
                   allow_small_or_imprecise_dtypes=True)
            pool.wait_ge(k_pool, 1)
            g.affine_select(out=head_mask[:], in_=head_mask[:], compare_op=ALU.is_ge, fill=0.0, base=HD - 1,
                            pattern=[[HD, HEADS], [0, HD]], channel_multiplier=-1).then_inc(k_pool, 1)

            def norm(dst, src, mv, rs, t):
                return g.tensor_scalar(dst[:, t, :], src[:, t, :], mv[:, t, 0:1], rs[:, t:t + 1],
                                       ALU.subtract, ALU.mult)

            def norm_x(b):
                pool.wait_ge(rstd1, b + 1)
                for t in range(TB * b, TB * (b + 1)):
                    last = norm(xn, xres, mv1, rs1, t)
                    if t % Q == Q - 1:
                        last.then_inc(xn_rdy, 1)

            def add_bo(c):
                pool.wait_ge(xn_rdy, c + 1)
                g.tensor_tensor(xres[:, Q * c:Q * c + Q, :], xres[:, Q * c:Q * c + Q, :],
                                b_o[:].unsqueeze(1).broadcast_to([P, Q, D]), ALU.add).then_inc(xb_rdy, 1)

            def scale_heads(b, col, r_col, done):
                pool.wait_ge(rn_rdy, b + 1)
                for h in range(QB):
                    v = qkv[:, b % 2, Q * h:Q * h + Q, col:col + D].rearrange("p j (n d) -> p j n d", d=HD)
                    r = rn[:, b % 2, Q * h:Q * h + Q, r_col:r_col + HEADS].unsqueeze(3).broadcast_to([P, Q, HEADS, HD])
                    g.tensor_tensor(v, v, r, ALU.mult).then_inc(done, 1)

            def norm_h(b):
                pool.wait_ge(rstd2, b + 1)
                for t in range(TB * b, TB * (b + 1)):
                    last = norm(xn, xres, mv2, rs2, t)
                    if t % Q == Q - 1:
                        last.then_inc(h_rdy, 1)

            for b in range(B):
                norm_x(b)
                if b == 0:
                    pool.wait_ge(ld_wa, 16 * 9)
            add_bo(0)
            add_bo(1)
            for b in range(1, B + 2):
                if b - 1 < B:
                    scale_heads(b - 1, 2 * D, HEADS, v_rdy)
                    scale_heads(b - 1, 0, 0, q_rdy)
                    if b < B:
                        add_bo(2 * b)
                        add_bo(2 * b + 1)
                if b >= 2:
                    norm_h(b - 2)

            pool.wait_ge(zero_st, 64)
            pool.wait_ge(pos_rdy, 1)
            for t in range(NT):
                pool.wait_ge(hs_rdy, t + 1)
                g.indirect_dma_start(out=x_slots, out_offset=bass.IndirectOffsetOnAxis(ap=pos[:, t:t + 1], axis=0),
                                     in_=xn[:, t, :], in_offset=None).then_inc(scat, 16)
            for s in yg_st:
                pool.wait_ge(s, 16 * NG // 2)
            for t in range(NT):
                g.indirect_dma_start(out=gath[:, t, :], out_offset=None, in_=y_slots,
                                     in_offset=bass.IndirectOffsetOnAxis(ap=pos[:, t:t + 1], axis=0)
                                     ).then_inc(gat[t // Q], 16)

        @block.scalar
        def _(act):
            a = nc.scalar
            for dst, src in ((w_qkv[:, 0:D], Wq), (w_qkv[:, D:2 * D], Wk), (w_qkv[:, 2 * D:QKV], Wv),
                             (b_qkv[:, 0:D], bq.partition_broadcast(P)), (b_qkv[:, D:2 * D], bk.partition_broadcast(P)),
                             (b_qkv[:, 2 * D:QKV], bv.partition_broadcast(P)), (b_o[:], bo.partition_broadcast(P)),
                             (w_o[:], Wo), (m_col[:], m.unsqueeze(1).broadcast_to([HEADS, HD]))):
                act.dma_start(dst, src).then_inc(ld_wa, 16)
            act.wait_ge(ld_wa, 16 * 9)
            act.wait_ge(z_done, 1)
            a.activation(m_tmp[:, 0:1], m_col[:], ACT.Exp, bias=zero_col[:], scale=-1.0).then_inc(ach, 1)
            act.wait_ge(m_step, 1)
            a.activation(m_tmp[:, 3:4], m_tmp[:, 2:3], ACT.Exp, bias=zero_col[:],
                         scale=-float(np.log(S))).then_inc(ach, 1)

            def std(dst, mv, var, done, b):
                act.wait_ge(var, b + 1)
                a.activation(dst[:, TB * b:TB * (b + 1)], mv[:, TB * b:TB * (b + 1), 1], ACT.Sqrt,
                             bias=eps_col[:], scale=1.0).then_inc(done, 1)

            copies = [0]

            def copy_T(dst):
                copies[0] += 1
                act.wait_ge(xT_mm, copies[0])
                a.copy(dst, ps_xT[:]).then_inc(xT_sb, 1)

            def xnT_copy(c):
                if c >= 2:
                    act.wait_ge(qkv_mm, 2 * (c - 1))
                copy_T(xnT[:, c % 2])

            def square(c):
                b, h = divmod(c, QB)
                act.wait_ge(qkv_sb, 2 * (c + 1))
                if c >= 2:
                    act.wait_ge(ss_done, c - 1)
                a.activation(sq[:, c % 2], qkv[:, b % 2, Q * h:Q * h + Q, 0:2 * D], ACT.Square).then_inc(sq_done, 1)

            def head_norms(b):
                act.wait_ge(ssum, b + 1)
                a.activation(rn[:, b % 2], ss[:, b % 2], ACT.Sqrt).then_inc(nrm, 1)

            def qT_copy(c):
                act.wait_ge(qT_mm, c + 1)
                if c >= 2:
                    act.wait_ge(y_mm, c - 1)
                a.copy(qT[:, c % 2], ps_qy[:]).then_inc(qT_sb, 1)

            def wb_copy(b):
                act.wait_ge(wb_mm, b + 1)
                if b >= 2:
                    act.wait_ge(y_mm, QB * (b - 1))
                a.copy(wb[:, b % 2], ps_vk[:, D:2 * D]).then_inc(wb_rdy, 1)

            def weights_copy(n):
                act.wait_ge(su_mm, n + 1)
                dst = (sgT[:], suT[:], sdT[:].rearrange("p k d -> p (k d)"), rwT[:])[n]
                a.copy(dst, setup_bank[:, 0:dst.shape[1]]).then_inc(su_cp, 1)

            for b in range(B):
                std(rs1, mv1, var1, std1, b)
            xnT_copy(0)
            xnT_copy(1)
            square(0)
            square(1)
            weights_copy(0)
            for b in range(1, B + 2):
                if b < B:
                    xnT_copy(2 * b)
                if b - 1 < B:
                    head_norms(b - 1)
                if b < B:
                    xnT_copy(2 * b + 1)
                    square(2 * b)
                    square(2 * b + 1)
                if b == 1:
                    weights_copy(1)
                if b - 1 < B:
                    qT_copy(2 * b - 2)
                    wb_copy(b - 1)
                    qT_copy(2 * b - 1)
                    std(rs2, mv2, var2, std2, b - 1)
                if b == 1:
                    weights_copy(2)
                    weights_copy(3)
                if b >= 2:
                    for c in (2 * b - 4, 2 * b - 3):
                        copy_T(hT[:, 512 * c:512 * c + 512])

            act.wait_ge(top_rdy, 1)
            a.activation(score[:], top[:], ACT.Sigmoid).then_inc(score_rdy, 1)
            act.wait_ge(score_rdy, 1)
            act.wait_ge(xT_mm, 2 * NQ)
            for t in range(NT):
                a.activation(xn[:, t, :], xn[:, t, :], ACT.Copy, scale=score[:, t:t + 1]).then_inc(hs_rdy, 1)

            def silu_shared(c, k):
                n = c * KC + k
                act.wait_ge(s_gu_mm, n + 1)
                a.activation(sg_act[:, k % 2], pair[:, 2 * (k % 2)], ACT.Silu).then_inc(s_silu, 1)

            def yT_copy(c):
                act.wait_ge(s_dn_end, c + 1)
                a.copy(yT[:], ps_yT[:]).then_inc(yT_sb, 1)

            def shared(lo, hi):
                for k in range(KC):
                    silu_shared(lo, k)
                with act.Fori(lo + 1, hi) as c:
                    silu_shared(c, 0)
                    yT_copy(c - 1)
                    for k in range(1, KC):
                        silu_shared(c, k)
                yT_copy(hi - 1)

            def experts(i, par, stages=(3, 2, 1, 0)):
                g = i * 2 + par
                if 3 in stages:
                    act.wait_ge(e_dn_mm, g - 2)
                    if not (isinstance(i, int) and g < 5):
                        act.wait_ge(yg_st[(par - 5) % 2], (i + (par - 5) // 2 + 1) * 16)
                    a.copy(yg[:, (par - 3) % 2].rearrange("p j d -> p (j d)"), ps_yg[:]).then_inc(yg_rdy, 1)
                if 1 in stages:
                    act.wait_ge(e_gu_mm, g)
                    a.activation(eg_act[:, (par - 1) % 2], gate_up_banks((par - 1) % 2)[:, :, 0:F],
                                 ACT.Silu).then_inc(e_silu, 1)
                if 0 in stages:
                    act.wait_ge(gT_mm, g + 1)
                    a.copy(xgT[:, par], ps_gT[:]).then_inc(gT_sb, 1)

            shared(0, C1)
            over_groups(experts, act)
            shared(C1, NQ)

        @block.vector
        def _(dve):
            v = nc.vector
            links = [0]

            def link(ins):
                links[0] += 1
                ins.then_inc(dch, 1)
                dve.wait_ge(dch, links[0])

            def stats(b, st, mv, done):
                for t in range(TB * b, TB * (b + 1)):
                    last = v.bn_stats(st[:, t, :], xres[:, t, :])
                link(last)
                for t in range(TB * b, TB * (b + 1)):
                    last = v.bn_aggr(mv[:, t, :], st[:, t, :])
                last.then_inc(done, 1)

            def inv_std(b, rs, std, done):
                dve.wait_ge(std, b + 1)
                v.reciprocal(rs[:, TB * b:TB * (b + 1)], rs[:, TB * b:TB * (b + 1)]).then_inc(done, 1)

            def take_qkv(c):
                b, h = divmod(c, QB)
                for j in (0, 2):
                    dve.wait_ge(qkv_mm, 2 * c + j // 2 + 1)
                    if c >= 4:
                        dve.wait_ge(qT_mm, c - 3)
                        dve.wait_ge(vk_mm, b - 1)
                    v.tensor_tensor(qkv[:, b % 2, Q * h + j:Q * h + j + 2, :], pair[:, j:j + 2, 0:QKV],
                                    b_qkv[:].unsqueeze(1).broadcast_to([P, 2, QKV]), ALU.add).then_inc(qkv_sb, 1)

            def head_sums(c):
                b, h = divmod(c, QB)
                dve.wait_ge(sq_done, c + 1)
                if c >= 4 and h == 0:
                    dve.wait_ge(nrm, b - 1)
                v.tensor_reduce(ss[:, b % 2, Q * h:Q * h + Q, :],
                                sq[:, c % 2].rearrange("p j (n d) -> p j n d", d=HD), AX.X, ALU.add
                                ).then_inc(ss_done, 1)

            def clamp_sums(b):
                dve.wait_ge(ss_done, QB * (b + 1))
                v.tensor_scalar(ss[:, b % 2], ss[:, b % 2], 1e-24, None, ALU.max).then_inc(ssum, 1)

            def inv_norms(b):
                dve.wait_ge(nrm, b + 1)
                v.reciprocal(rn[:, b % 2], rn[:, b % 2]).then_inc(rn_rdy, 1)

            def mask_vk(b):
                dve.wait_ge(vk_mm, b + 1)
                if b >= 2:
                    dve.wait_ge(wb_mm, b - 1)
                v.tensor_tensor(vkm[:, b % 2], ps_vk[:, 0:D], head_mask[:], ALU.mult).then_inc(vkm_rdy, 1)

            def add_attn(c):
                dve.wait_ge(y_mm, c + 1)
                dve.wait_ge(xb_rdy, c + 1)
                r = xres[:, Q * c:Q * c + Q, :]
                v.tensor_tensor(r, ps_qy[:].rearrange("p (j d) -> p j d", d=D), r, ALU.add).then_inc(x1_rdy, 1)

            dve.wait_ge(ld_x0, 16)
            stats(0, st1, mv1, var1)
            dve.wait_ge(ach, 1)
            link(v.tensor_scalar(m_tmp[:, 1:2], m_tmp[:, 0:1], 1.0, None, ALU.add))
            v.reciprocal(m_tmp[:, 2:3], m_tmp[:, 1:2]).then_inc(m_step, 1)
            inv_std(0, rs1, std1, rstd1)
            dve.wait_ge(ld_x, 16 * (B - 1))
            for b in range(1, B):
                stats(b, st1, mv1, var1)
                inv_std(b, rs1, std1, rstd1)
                if b == 1:
                    dve.wait_ge(ach, 2)
                    dve.wait_ge(k_pool, 2)
                    link(v.tensor_scalar(head_mask[:], head_mask[:], m_tmp[:, 3:4], None, ALU.mult))
            take_qkv(0)
            take_qkv(1)
            head_sums(0)
            head_sums(1)
            clamp_sums(0)
            for b in range(1, B + 2):
                if b < B:
                    take_qkv(2 * b)
                if b - 1 < B:
                    inv_norms(b - 1)
                if b >= 2:
                    inv_std(b - 2, rs2, std2, rstd2)
                if b < B:
                    head_sums(2 * b)
                    take_qkv(2 * b + 1)
                if b - 1 < B:
                    mask_vk(b - 1)
                if b < B:
                    head_sums(2 * b + 1)
                    clamp_sums(b)
                if b - 1 < B:
                    add_attn(2 * b - 2)
                    add_attn(2 * b - 1)
                    dve.wait_ge(x1_rdy, QB * b)
                    stats(b - 1, st2, mv2, var2)

            v.engine_nop().then_inc(y_free, 1)
            dve.wait_ge(log_mm, NQ)
            dve.wait_ge(k_pool, 2)
            logits = ps_log[:].rearrange("p (t e) -> p t e", e=E)
            v.tensor_reduce(top[:], logits, AX.X, ALU.max).then_inc(top_rdy, 1)
            dve.wait_ge(top_rdy, 1)
            link(v.tensor_tensor(key[:], logits, top[:].unsqueeze(2).broadcast_to([P, NT, E]), ALU.is_equal))
            link(v.tensor_tensor(key[:], key[:], rank_key[:], ALU.mult))
            link(v.tensor_reduce(ktop[:], key[:], AX.X, ALU.max))
            link(v.tensor_tensor(hot[:].rearrange("p e t -> p t e"), key[:],
                                 ktop[:].unsqueeze(2).broadcast_to([P, NT, E]), ALU.is_equal))
            v.tensor_reduce(cnt[:], hot[:], AX.X, ALU.add).then_inc(cnt_rdy, 1)
            link(v.tensor_tensor_scan(run[:].rearrange("p e t -> p (e t)"), run_mask[:].rearrange("p e t -> p (e t)"),
                                      hot[:].rearrange("p e t -> p (e t)"), 0.0, ALU.mult, ALU.add))
            dve.wait_ge(cnt_mm, 1)
            link(v.tensor_scalar(tot_i[:], ps_vk[:, 32:32 + E], float(P - 1), None, ALU.add))
            link(v.tensor_scalar(til_i[:], tot_i[:], P.bit_length() - 1, None, ALU.logical_shift_right))
            link(v.tensor_copy(til[:], til_i[:]))
            link(v.tensor_tensor_scan(til_end[:], ones[:, 0:E], til[:], 0.0, ALU.mult, ALU.add))
            link(v.tensor_tensor(base[:], til_end[:], til[:], ALU.subtract))
            link(v.tensor_scalar(base[:], base[:], float(P), -1.0, ALU.mult, ALU.add))
            link(v.tensor_tensor(base[:], ps_vk[:, 0:E], base[:], ALU.add))
            link(v.tensor_tensor(run[:], run[:], base[:].unsqueeze(2).broadcast_to([P, E, NT]), ALU.add))
            link(v.tensor_tensor(run[:], run[:], hot[:], ALU.mult))
            link(v.tensor_reduce(pos_f[:], run[:].rearrange("p e t -> p t e"), AX.X, ALU.add))
            v.tensor_copy(pos[:], pos_f[:]).then_inc(pos_rdy, 1)
            link(v.tensor_tensor(past[:], til_end[0:1, :].unsqueeze(1).broadcast_to([1, SLOT_TILES, E]), tile_no[:],
                                 ALU.is_le))
            link(v.tensor_reduce(eid_f[:], past[:], AX.X, ALU.add))
            v.tensor_scalar(eid[:], eid_f[:], float(E - 1), float(WE), ALU.min, ALU.mult).then_inc(eid_rdy, 1)

            def act_shared(c, k):
                dve.wait_ge(s_silu, c * KC + k + 1)
                v.tensor_tensor(s_act[:, k % 2], pair[:, 2 * (k % 2) + 1], sg_act[:, k % 2], ALU.mult
                                ).then_inc(s_act_rdy, 1)

            def add_shared(c):
                dve.wait_ge(yT_mm, c + 1)
                r = xres[:, bass.ds(c * Q, Q), :]
                v.tensor_tensor(r, ps_y[:].rearrange("p (j d) -> p j d", d=D), r, ALU.add).then_inc(y_free, 1)

            def shared(lo, hi):
                for k in range(KC):
                    act_shared(lo, k)
                with dve.Fori(lo + 1, hi) as c:
                    act_shared(c, 0)
                    act_shared(c, 1)
                    add_shared(c - 1)
                    act_shared(c, 2)
                    act_shared(c, 3)
                add_shared(hi - 1)

            def experts(i, par, stages=(3, 2, 1, 0)):
                g = i * 2 + par
                if 2 in stages:
                    dve.wait_ge(aT_mm, g - 1)
                    v.tensor_copy(e_actT[:, par], ps_aT[:]).then_inc(aT_sb, 1)
                if 1 in stages:
                    dve.wait_ge(e_silu, g)
                    v.tensor_tensor(e_act[:, (par - 1) % 2], gate_up_banks((par - 1) % 2)[:, :, F:F2],
                                    eg_act[:, (par - 1) % 2], ALU.mult).then_inc(e_act_rdy, 1)

            shared(0, C1)
            over_groups(experts, dve)
            shared(C1, NQ)
            for c in range(NQ):
                dve.wait_ge(gat[c], 16 * Q)
                dve.wait_ge(y_free, NQ + 1)
                r = gath[:, Q * c:Q * c + Q, :]
                v.tensor_tensor(r, r, xres[:, Q * c:Q * c + Q, :], ALU.add).then_inc(fin, 1)

        @block.tensor
        def _(pe):
            te = nc.tensor
            pe.wait_ge(k_id, 1)
            turned = [0]

            def turn(src, c, ready):
                pe.wait_ge(ready, c + 1)
                if turned[0]:
                    pe.wait_ge(xT_sb, turned[0])
                turned[0] += 1
                for j, t in enumerate(tiles(c)):
                    last = te.transpose(ps_xT[:, P * j:P * j + P], src[:, t, :], ident[:])
                last.then_inc(xT_mm, 1)

            def project(c):
                if c == 0:
                    pe.wait_ge(ld_wa, 16 * 9)
                pe.wait_ge(xT_sb, copy_of_xn[c])
                for j in range(Q):
                    if j % 2 == 0 and c >= 1:
                        pe.wait_ge(qkv_sb, 2 * (c - 1) + j // 2 + 1)
                    last = te.matmul(pair[:, j, 0:QKV], xnT[:, c % 2, P * j:P * j + P], w_qkv[:], start=True, stop=True)
                    if j % 2:
                        last.then_inc(qkv_mm, 1)

            def v_by_k(b):
                if b >= 1:
                    pe.wait_ge(wb_rdy, b)
                for t in range(TB):
                    if t % Q == 0:
                        pe.wait_ge(v_rdy, QB * b + t // Q + 1)
                    last = te.matmul(ps_vk[:, 0:D], qkv[:, b % 2, t, 2 * D:QKV], qkv[:, b % 2, t, D:2 * D],
                                     start=(t == 0), stop=(t == TB - 1))
                last.then_inc(vk_mm, 1)

            def fold_wo(b):
                pe.wait_ge(vkm_rdy, b + 1)
                te.matmul(ps_vk[:, D:2 * D], vkm[:, b % 2], w_o[:], start=True, stop=True).then_inc(wb_mm, 1)

            def turn_q(c):
                b, h = divmod(c, QB)
                pe.wait_ge(q_rdy, c + 1)
                if c >= 1:
                    pe.wait_ge(x1_rdy, c)
                for j in range(Q):
                    last = te.transpose(ps_qy[:, P * j:P * j + P], qkv[:, b % 2, Q * h + j, 0:D], ident[:])
                last.then_inc(qT_mm, 1)

            def attend(c):
                pe.wait_ge(qT_sb, c + 1)
                pe.wait_ge(wb_rdy, c // QB + 1)
                for j in range(Q):
                    last = te.matmul(ps_qy[:, P * j:P * j + P], qT[:, c % 2, P * j:P * j + P], wb[:, c // QB % 2],
                                     start=True, stop=True)
                last.then_inc(y_mm, 1)

            def route(c):
                pe.wait_ge(xT_sb, turned[0])
                for t in tiles(c):
                    last = te.matmul(ps_log[:, E * t:E * t + E], hT[:, P * t:P * t + P], rwT[:], start=True, stop=True)
                last.then_inc(log_mm, 1)

            def turn_weights(n):
                if n == 0:
                    pe.wait_ge(ld_ws, 16 * 4)
                else:
                    pe.wait_ge(su_cp, n)
                if n == 3:
                    last = te.transpose(setup_bank[:, 0:E], rw_in[:], ident[0:E, 0:E])
                else:
                    for k in range(KC):
                        src = (sg_in[:, k, :], su_in[:, k, :], sd_in[:, P * k:P * k + P])[n]
                        last = te.transpose(setup_bank[:, P * k:P * k + P], src, ident[:])
                last.then_inc(su_mm, 1)

            copy_of_xn = {}
            for c in (0, 1):
                turn(xn, c, xn_rdy)
                copy_of_xn[c] = turned[0]
            project(0)
            project(1)
            turn_weights(0)
            for b in range(1, B + 2):
                if b < B:
                    for c in (2 * b, 2 * b + 1):
                        turn(xn, c, xn_rdy)
                        copy_of_xn[c] = turned[0]
                    project(2 * b)
                    project(2 * b + 1)
                if b == 1:
                    turn_weights(1)
                if b - 1 < B:
                    v_by_k(b - 1)
                    turn_q(2 * b - 2)
                    fold_wo(b - 1)
                    attend(2 * b - 2)
                    turn_q(2 * b - 1)
                    attend(2 * b - 1)
                if b == 1:
                    turn_weights(2)
                    turn_weights(3)
                    pe.wait_ge(su_cp, 4)
                if b >= 2:
                    for c in (2 * b - 4, 2 * b - 3):
                        turn(xn, c, h_rdy)
                        route(c)

            pe.wait_ge(cnt_rdy, 1)
            te.matmul(ps_vk[:, 0:E], before[:], cnt[:], start=True, stop=True)
            te.matmul(ps_vk[:, 32:32 + E], ones[:], cnt[:], start=True, stop=True).then_inc(cnt_mm, 1)

            def gate_up_shared(c, k, first=False):
                n = c * KC + k
                if not (first and k < 2):
                    pe.wait_ge(s_act_rdy, n - 1)
                h = hT[:, bass.ds(c * 512, 512)]
                te.matmul(pair[:, 2 * (k % 2)], sgT[:, P * k:P * k + P], h, start=True, stop=True)
                te.matmul(pair[:, 2 * (k % 2) + 1], suT[:, P * k:P * k + P], h, start=True, stop=True
                          ).then_inc(s_gu_mm, 1)

            def down_shared(c, k):
                pe.wait_ge(s_act_rdy, c * KC + k + 1)
                if k == 0 and not (isinstance(c, int) and c == 0):
                    pe.wait_ge(yT_sb, c)
                mm = te.matmul(ps_yT[:], sdT[:, k, :], s_act[:, k % 2], start=(k == 0), stop=(k == KC - 1))
                if k == KC - 1:
                    mm.then_inc(s_dn_end, 1)

            def turn_y(c, first=False):
                pe.wait_ge(yT_sb, c + 1)
                pe.wait_ge(y_free, c + 1)
                for j in range(Q):
                    last = te.transpose(ps_y[:, P * j:P * j + P], yT[:, P * j:P * j + P], ident[:])
                last.then_inc(yT_mm, 1)

            def shared(lo, hi):
                gate_up_shared(lo, 0, lo == 0)
                for k in range(1, KC):
                    gate_up_shared(lo, k, lo == 0)
                    down_shared(lo, k - 1)
                with pe.Fori(lo + 1, hi) as c:
                    gate_up_shared(c, 0)
                    down_shared(c - 1, KC - 1)
                    gate_up_shared(c, 1)
                    down_shared(c, 0)
                    turn_y(c - 1)
                    for k in range(2, KC):
                        gate_up_shared(c, k)
                        down_shared(c, k - 1)
                down_shared(hi - 1, KC - 1)
                turn_y(hi - 1)

            def columns(g):
                _, vals = nc.values_load_multi_w_load_instructions(
                    eid[0:1, bass.ds(g * Q, Q)], engines=(mybir.EngineType.PE,), min_val=0, max_val=(E - 1) * WE)
                return vals

            w_cols = w_e[:].rearrange("p e c -> p (e c)")

            def experts(i, par, stages=(3, 2, 1, 0)):
                g = i * 2 + par
                if 3 in stages:
                    cols = columns(g - 3)
                    pe.wait_ge(aT_sb, g - 2)
                    if not (isinstance(g, int) and g == 3):
                        pe.wait_ge(yg_rdy, g - 3)
                    for j in range(Q):
                        mm = te.matmul(ps_yg[:, P * j:P * j + P], e_actT[:, (par - 3) % 2, P * j:P * j + P],
                                       w_cols[:, bass.ds(cols[j] + F2, D)], start=True, stop=True)
                    mm.then_inc(e_dn_mm, 1)
                if 2 in stages:
                    pe.wait_ge(e_act_rdy, g - 1)
                    if not (isinstance(g, int) and g == 2):
                        pe.wait_ge(aT_sb, g - 2)
                    for j in range(Q):
                        mm = te.transpose(ps_aT[:, P * j:P * j + P], e_act[:, par, j, :], ident[:])
                    mm.then_inc(aT_mm, 1)
                if 1 in stages:
                    cols = columns(g - 1)
                    pe.wait_ge(gT_sb, g)
                    for j in range(Q):
                        mm = te.matmul(gate_up_banks((par - 1) % 2)[:, j, :], xgT[:, (par - 1) % 2, P * j:P * j + P],
                                       w_cols[:, bass.ds(cols[j], F2)], start=True, stop=True)
                    mm.then_inc(e_gu_mm, 1)
                if 0 in stages:
                    pe.wait_ge(xg_ld[par], (i + 1) * 16)
                    if not (isinstance(g, int) and g == 0):
                        pe.wait_ge(gT_sb, g)
                    for j in range(Q):
                        mm = te.transpose(ps_gT[:, P * j:P * j + P], xg[:, par, j, :], ident[:])
                    mm.then_inc(gT_mm, 1)

            shared(0, C1)
            pe.wait_ge(eid_rdy, 1)
            pe.wait_ge(ld_we, 32)
            over_groups(experts, pe)
            shared(C1, NQ)


_INS = ["L0_attn_x", "L0_attn_Wq", "L0_attn_bq", "L0_attn_Wk", "L0_attn_bk", "L0_attn_Wv", "L0_attn_bv", "L0_attn_Wo",
        "L0_attn_bo", "L0_attn_m", "L0_ffn_router_w", "L0_ffn_gate_up_proj", "L0_ffn_down_proj",
        "L0_ffn_shared_gate_w", "L0_ffn_shared_up_w", "L0_ffn_shared_down_w"]


def kernel(**inputs):
    import concourse.bacc as bacc
    from concourse.bass_utils import run_bass_kernel_spmd

    nc = bacc.Bacc("TRN2", target_bir_lowering=False, num_devices=1)
    arrays = {name: np.ascontiguousarray(inputs[name]) for name in _INS}
    args = [nc.dram_tensor(name, a.shape, F32, kind="ExternalInput").ap() for name, a in arrays.items()]
    out = nc.dram_tensor("out", arrays["L0_attn_x"].shape, F32, kind="ExternalOutput").ap()
    build_block(nc, *args, out)
    return run_bass_kernel_spmd(nc, [arrays], core_ids=[0]).results[0]["out"]
```

```python
from contextlib import ExitStack

import numpy as np

import concourse.bass as bass
from concourse import mybir

ALU = mybir.AluOpType
ACT = mybir.ActivationFunctionType
AX = mybir.AxisListType
F32 = mybir.dt.float32
F32R = mybir.dt.float32r
I32 = mybir.dt.int32

P = 128


def build_block(nc, x, Wq, bq, Wk, bk, Wv, bv, Wo, bo, m, router_w, gate_up, down, shared_gate, shared_up,
                shared_down, out):
    B, S, D = x.shape
    HEADS = m.shape[0]
    HD = D // HEADS
    E, _, F2 = gate_up.shape
    F = F2 // 2
    SF = shared_gate.shape[0]
    T = B * S
    NT = T // P
    TB = S // P
    Q = 4
    NQ = NT // Q
    QB = TB // Q
    KC = SF // P
    NG = -(-(NT + E - 1) // Q)
    SLOT_TILES = NG * Q
    SLOTS = SLOT_TILES * P
    QKV = 3 * D
    W = D + 1
    QRING = 2
    RING = 3
    EPS = 1e-5
    EC = 4
    C1 = 5
    ZERO_LOADS = 8
    ZW = SLOT_TILES * W // ZERO_LOADS
    POOL_FINAL = NQ - 2
    POOL_QUADS = 6
    assert D == P and F == P and QB == 2 and NG == 12 and KC == 4

    x_slots = nc.dram_tensor("x_slots", (SLOTS, W), F32, kind="Internal").ap()
    y_rows = nc.dram_tensor("y_rows", (1 + T + SLOTS, D), F32, kind="Internal").ap()
    x_rows = x.rearrange("b (j p) d -> p (b j) d", p=P)
    out_rows = out.rearrange("b (j p) d -> p (b j) d", p=P)

    with ExitStack() as ctx:
        def sb(name, shape, dt=F32):
            return ctx.enter_context(nc.sbuf_tensor(name, shape, dt))

        def sem(name):
            return ctx.enter_context(nc.semaphore(name))

        xres = sb("xres", [P, NT, D])
        h_rows = sb("h_rows", [P, NT, W])
        hT = sb("hT", [P, 2, T], F32R)
        st1 = sb("st1", [P, NT, 6])
        mv1 = sb("mv1", [P, NT, 2])
        rs1 = sb("rs1", [P, NT])
        nm2 = sb("nm2", [P, NT])
        st2 = sb("st2", [P, NT, 6])
        mv2 = sb("mv2", [P, NT, 2])
        rs2 = sb("rs2", [P, NT])
        w_o = sb("w_o", [P, D])
        ident = sb("ident", [P, P])
        before = sb("before", [P, P])
        ones = sb("ones", [P, P])
        eps_col = sb("eps_col", [P, 1])
        zero_col = sb("zero_col", [P, 1])
        rwT = sb("rwT", [P, 2, E], F32R)
        sgT = sb("sgT", [P, 2, SF], F32R)
        suT = sb("suT", [P, 2, SF], F32R)
        sdT = sb("sdT", [P, 2, KC * D], F32R)
        w_gu = sb("w_gu", [P, 2, E, F2], F32R)
        w_dn = sb("w_dn", [P, E, D])
        sg_act = sb("sg_act", [P, 2, 512])
        s_act = sb("s_act", [P, 2, 512])
        s_spl = sb("s_spl", [P, 2, 2, 512], F32R)
        yT = sb("yT", [P, 512])
        top = sb("top", [P, NT])
        score = sb("score", [P, NT])
        cnt = sb("cnt", [P, E])
        tot_i = sb("tot_i", [P, E], I32)
        til_i = sb("til_i", [P, E], I32)
        til = sb("til", [P, E])
        til_end = sb("til_end", [P, E])
        base = sb("base", [P, E])
        pos_f = sb("pos_f", [P, NT])
        pos = sb("pos", [P, NT], I32)
        eid_f = sb("eid_f", [1, SLOT_TILES])
        eid = sb("eid", [1, NG + 3, 2, Q], I32)
        rank_key = sb("rank_key", [P, NT, E])
        free_row = sb("free_row", [P, SLOT_TILES])
        run_mask = sb("run_mask", [P, E, NT])
        tile_no = sb("tile_no", [1, SLOT_TILES, E])

        with ExitStack() as attention:
            def sb_a(name, shape, dt=F32):
                return attention.enter_context(nc.sbuf_tensor(name, shape, dt))

            w_raw = sb_a("w_raw", [P, 2, EC, F2])
            qkv = sb_a("qkv", [P, QRING, Q, QKV])
            sq = sb_a("sq", [P, Q, 2 * D])
            xT = sb_a("xT", [P, 2, Q * P])
            hT_raw = sb_a("hT_raw", [P, 2, Q * P])
            qT = sb_a("qT", [P, RING, Q * P])
            ss = sb_a("ss", [P, 2, Q, 2 * HEADS])
            rn = sb_a("rn", [P, 2, Q, 2 * HEADS])
            vkm = sb_a("vkm", [P, 2, D])
            wb = sb_a("wb", [P, 2, D])
            w_qkv = sb_a("w_qkv", [P, QKV])
            b_qkv = sb_a("b_qkv", [P, QKV])
            center = sb_a("center", [P, P])
            w_c = sb_a("w_c", [P, QKV])
            b_o = sb_a("b_o", [P, D])
            m_col = sb_a("m_col", [P, 1])
            m_tmp = sb_a("m_tmp", [P, 4])
            head_mask = sb_a("head_mask", [P, D])
            rw_in = sb_a("rw_in", [E, D])
            sg_in = sb_a("sg_in", [P, KC, D])
            su_in = sb_a("su_in", [P, KC, D])
            sd_in = sb_a("sd_in", [P, SF])
        xgT = sb("xgT", [P, 2, 2, Q * P], F32R)
        e_actT = sb("e_actT", [P, 2, Q * P])
        xg = sb("xg", [P, 2, Q, W])
        eg_act = sb("eg_act", [P, 2, Q, F])
        e_act = sb("e_act", [P, 2, Q, F])
        yg = sb("yg", [P, SLOT_TILES, D])
        home = sb("home", [P, SLOT_TILES], I32)
        away = sb("away", [P, SLOT_TILES])
        key = sb("key", [P, NT, E])
        ktop = sb("ktop", [P, NT])
        hot = sb("hot", [P, E, NT])
        run = sb("run", [P, E, NT])
        past = sb("past", [1, SLOT_TILES, E])

        bank = [ctx.enter_context(nc.psum_tensor(f"bank{i}", [P, 512], F32)) for i in range(4)]
        pair = ctx.enter_context(nc.psum_tensor("quad_banks", [P, 4, 512], F32))
        ps_xT, ps_qy, ps_vk, ps_log = bank
        ps_yT, ps_y = bank[0], bank[1]
        ps_gT, ps_aT, ps_yg = bank[3], bank[1], bank[2]
        setup_bank = bank[3]

        ld_x = [sem(f"ld_x{c}") for c in range(NQ)]
        ld_we = [sem(f"ld_we{n}") for n in range(E // EC)]
        ld_wd, ld_m = sem("ld_wd"), sem("ld_m")
        ld_b, ld_wo = sem("ld_b"), sem("ld_wo")
        ld_wa, ld_ws = sem("ld_wa"), sem("ld_ws")
        we_hi, we_lo = sem("we_hi"), sem("we_lo")
        k_ids = sem("k_ids")
        k_col, k_id, k_pool = sem("k_col"), sem("k_id"), sem("k_pool")
        z_done, zero_st = sem("z_done"), sem("zero_st")
        dch = sem("dch")
        ach = sem("ach")
        m_step = sem("m_step")
        var1, std1, rstd1 = sem("var1"), sem("std1"), sem("rstd1")
        center_rdy, wc_mm, wc_rdy, bo_add = sem("center_rdy"), sem("wc_mm"), sem("wc_rdy"), sem("bo_add")
        xT_mm, xT_sb = sem("xT_mm"), sem("xT_sb")
        qkv_mm, qkv_sb, sq_done, ss_done = sem("qkv_mm"), sem("qkv_sb"), sem("sq_done"), sem("ss_done")
        ssum, nrm, rn_rdy = sem("ssum"), sem("nrm"), sem("rn_rdy")
        v_rdy, q_rdy = sem("v_rdy"), sem("q_rdy")
        vk_mm, vkm_rdy, wb_mm, wb_rdy = sem("vk_mm"), sem("vkm_rdy"), sem("wb_mm"), sem("wb_rdy")
        qT_mm, qT_sb, y_mm, x1_rdy = sem("qT_mm"), sem("qT_sb"), sem("y_mm"), sem("x1_rdy")
        var2, std2, rstd2, h_rdy = sem("var2"), sem("std2"), sem("rstd2"), sem("h_rdy")
        su_mm, su_cp, su_lo, log_mm = sem("su_mm"), sem("su_cp"), sem("su_lo"), sem("log_mm")
        hT_hi_rdy, hT_rdy = sem("hT_hi_rdy"), sem("hT_rdy")
        top_rdy, score_rdy, hs_rdy, cnt_rdy, cnt_mm, pos_rdy, eid_rdy = (
            sem("top_rdy"), sem("score_rdy"), sem("hs_rdy"), sem("cnt_rdy"), sem("cnt_mm"), sem("pos_rdy"),
            sem("eid_rdy"))
        hs_pool, scat = sem("hs_pool"), sem("scat")
        s_gu_mm, s_silu, s_act_rdy, s_hi, s_spl_rdy, s_dn_mm = (
            sem("s_gu_mm"), sem("s_silu"), sem("s_act_rdy"), sem("s_hi"), sem("s_spl_rdy"), sem("s_dn_mm"))
        yT_sb, yT_mm, y_free = sem("yT_sb"), sem("yT_mm"), sem("y_free")
        xg_ld = [sem("xg_ld0"), sem("xg_ld1")]
        gT_mm, gT_sb, e_gu_mm, e_silu, e_act_rdy = (
            sem("gT_mm"), sem("gT_sb"), sem("e_gu_mm"), sem("e_silu"), sem("e_act_rdy"))
        gT_hi = sem("gT_hi")
        aT_mm, aT_sb, e_dn_mm, yg_rdy = sem("aT_mm"), sem("aT_sb"), sem("e_dn_mm"), sem("yg_rdy")
        away_rdy, home_rdy, back = sem("away_rdy"), sem("home_rdy"), sem("back")
        ld_y = [sem(f"ld_y{c}") for c in range(NQ)]
        fin_pool = sem("fin_pool")
        fin, out_st = sem("fin"), sem("out_st")

        block = ctx.enter_context(nc.Block())

        def tiles(c):
            return range(Q * c, Q * c + Q)

        STEPS = NQ + 4
        SPLIT_STEPS = (2, 4, 6, 8)

        def live(c):
            return 0 <= c < NQ

        turns = [("x", 0)] + [(kind, c) for s in range(STEPS) for kind, c in (("h", s - 4), ("x", s + 1)) if live(c)]
        turn_no = {turn: n + 1 for n, turn in enumerate(turns)}

        def slots(dram, g):
            return dram[bass.ds(g * (Q * P), Q * P), :].rearrange("(j p) d -> p j d", p=P)

        def gate_up_banks(par):
            return pair[:, 2 * par:2 * par + 2, :].rearrange("p a (b n) -> p (a b) n", b=2)

        def over_groups(step, eng, filler=lambda k: None):
            step(0, 1, (1, 0))
            step(1, 0, (2, 1, 0))
            step(1, 1, (3, 2, 1, 0))
            step(2, 0)
            step(2, 1)
            with eng.Fori(3, NG // 2) as i:
                step(i, 0)
                step(i, 1)
            step(NG // 2, 0, (3, 2, 1))
            filler(0)
            step(NG // 2, 1, (3, 2))
            filler(1)
            step(NG // 2 + 1, 0, (3,))

        @block.sync
        def _(sp):
            for c in range(NQ):
                sp.dma_start(xres[:, Q * c:Q * c + Q, :], x_rows[:, Q * c:Q * c + Q, :]).then_inc(ld_x[c], 16)
                if c == 0:
                    for n, b in enumerate((bq, bk, bv)):
                        sp.dma_start(b_qkv[:, D * n:D * n + D], b.partition_broadcast(P)).then_inc(ld_b, 16)
                if c == 1:
                    sp.dma_start(b_o[:], bo.partition_broadcast(P)).then_inc(ld_wo, 16)
                    sp.dma_start(w_o[:], Wo).then_inc(ld_wo, 16)
            sp.dma_start(sg_in[:], shared_gate.rearrange("(k f) h -> f k h", f=P)).then_inc(ld_ws, 16)
            sp.dma_start(su_in[:], shared_up.rearrange("(k f) h -> f k h", f=P)).then_inc(ld_ws, 16)
            sp.dma_start(sd_in[:], shared_down).then_inc(ld_ws, 16)
            sp.dma_start(rw_in[:], router_w).then_inc(ld_ws, 16)
            sp.wait_ge(z_done, 1)
            rows = x_slots.rearrange("(p r) d -> p (r d)", p=P)
            zeros = w_raw[:, 1].rearrange("p e n -> p (e n)")
            for i in range(ZERO_LOADS):
                sp.dma_start(rows[:, i * ZW:(i + 1) * ZW], zeros[:, 0:ZW]).then_inc(zero_st, 16)
            for n in range(E // EC):
                if n == 1:
                    sp.wait_ge(zero_st, 16 * ZERO_LOADS)
                if n >= 2:
                    sp.wait_ge(we_lo, n - 1)
                e = slice(n * EC, n * EC + EC)
                sp.dma_start(w_raw[:, n % 2], gate_up[e].rearrange("e h f -> h e f")).then_inc(ld_we[n], 16)
            sp.dma_start(w_dn[:], down.rearrange("e f h -> f e h")).then_inc(ld_wd, 16)

            def load_group(g, par):
                sp.dma_start(xg[:, par], slots(x_slots, g)).then_inc(xg_ld[par], 16)

            def experts(i, par, stages=(3, 2, 1, 0)):
                g = i * 2 + par
                if 0 in stages:
                    if not (isinstance(i, int) and g < 2):
                        sp.wait_ge(gT_mm, g - 1)
                        sp.wait_ge(home_rdy, g - 1)
                    load_group(g, par)

            sp.wait_ge(scat, 16 * NT)
            experts(0, 0, (0,))
            over_groups(experts, sp)
            sp.wait_ge(back, 16 * SLOT_TILES)
            y_home = y_rows[1:1 + T, :].rearrange("(j p) d -> p j d", p=P)
            for c in range(NQ):
                sp.dma_start(h_rows[:, Q * c:Q * c + Q, 0:D], y_home[:, Q * c:Q * c + Q, :]).then_inc(ld_y[c], 16)
            for c in range(NQ):
                if c < POOL_FINAL:
                    sp.wait_ge(fin_pool, c + 1)
                else:
                    sp.wait_ge(fin, c - POOL_FINAL + 1)
                sp.dma_start(out_rows[:, Q * c:Q * c + Q, :], xres[:, Q * c:Q * c + Q, :]).then_inc(out_st, 16)
            sp.wait_ge(out_st, 16 * NQ)

        @block.gpsimd
        def _(pool):
            g = nc.gpsimd
            g.memset(eps_col[:], EPS)
            g.memset(zero_col[:], 0.0).then_inc(k_col, 1)
            g.memset(ident[:], 0.0)
            g.memset(before[:], 1.0)
            g.memset(ones[:], 1.0)
            g.memset(head_mask[:], 1.0)
            g.memset(run_mask[:], 1.0)
            g.memset(w_raw[:, 1], 0.0).then_inc(z_done, 1)
            pool.wait_ge(z_done, 1)
            g.affine_select(out=ident[:], in_=ident[:], compare_op=ALU.not_equal, fill=1.0, base=0,
                            pattern=[[-1, P]], channel_multiplier=1).then_inc(k_id, 1)
            g.affine_select(out=before[:], in_=before[:], compare_op=ALU.is_gt, fill=0.0, base=0,
                            pattern=[[1, P]], channel_multiplier=-1)
            g.affine_select(out=head_mask[:], in_=head_mask[:], compare_op=ALU.is_ge, fill=0.0, base=0,
                            pattern=[[-HD, HEADS], [0, HD]], channel_multiplier=1).then_inc(k_pool, 1)
            g.affine_select(out=run_mask[:], in_=run_mask[:], compare_op=ALU.not_equal, fill=0.0, base=0,
                            pattern=[[0, E], [1, NT]], channel_multiplier=0)
            g.iota(h_rows[:, :, D], pattern=[[P, NT]], base=1, channel_multiplier=1,
                   allow_small_or_imprecise_dtypes=True).then_inc(k_ids, 1)
            g.iota(free_row[:], pattern=[[P, SLOT_TILES]], base=1 + T, channel_multiplier=1,
                   allow_small_or_imprecise_dtypes=True).then_inc(k_ids, 1)
            g.iota(rank_key[:], pattern=[[0, NT], [-1, E]], base=E, channel_multiplier=0,
                   allow_small_or_imprecise_dtypes=True)
            g.iota(tile_no[:], pattern=[[1, SLOT_TILES], [0, E]], base=0, channel_multiplier=0,
                   allow_small_or_imprecise_dtypes=True)
            pool.wait_ge(k_pool, 1)
            g.affine_select(out=head_mask[:], in_=head_mask[:], compare_op=ALU.is_ge, fill=0.0, base=HD - 1,
                            pattern=[[HD, HEADS], [0, HD]], channel_multiplier=-1).then_inc(k_pool, 1)

            def scale_heads(c, col, r_col, done):
                pool.wait_ge(rn_rdy, c + 1)
                v = qkv[:, c % QRING, :, col:col + D].rearrange("p j (n d) -> p j n d", d=HD)
                r = rn[:, c % 2, :, r_col:r_col + HEADS].unsqueeze(3).broadcast_to([P, Q, HEADS, HD])
                g.tensor_tensor(v, v, r, ALU.mult).then_inc(done, 1)

            def add_bo(c):
                if c == 0:
                    pool.wait_ge(ld_wo, 16 * 2)
                pool.wait_ge(var1, c + 1)
                pool.wait_ge(xT_mm, turn_no["x", c])
                r = xres[:, Q * c:Q * c + Q, :]
                g.tensor_tensor(r, r, b_o[:].unsqueeze(1).broadcast_to([P, Q, D]), ALU.add).then_inc(bo_add, 1)

            def hT_lo(c):
                pool.wait_ge(hT_hi_rdy, c + 1)
                g.tensor_tensor(hT[:, 1, 512 * c:512 * c + 512], hT_raw[:, c % 2],
                                hT[:, 0, 512 * c:512 * c + 512].bitcast(F32), ALU.subtract).then_inc(hT_rdy, 1)

            def split_lo(n):
                e = slice(n * EC, n * EC + EC)
                pool.wait_ge(we_hi, n + 1)
                g.tensor_tensor(w_gu[:, 1, e, :], w_raw[:, n % 2], w_gu[:, 0, e, :].bitcast(F32), ALU.subtract
                                ).then_inc(we_lo, 1)

            for s in range(STEPS):
                if live(s - 1):
                    scale_heads(s - 1, 2 * D, HEADS, v_rdy)
                    scale_heads(s - 1, 0, 0, q_rdy)
                if live(s - 4):
                    hT_lo(s - 4)
                if live(s - 1):
                    add_bo(s - 1)
                if s in SPLIT_STEPS:
                    split_lo(SPLIT_STEPS.index(s))

            pool.wait_ge(score_rdy, 1)
            pool.wait_ge(xT_mm, 2 * NQ)
            for c in range(POOL_QUADS):
                t = slice(Q * c, Q * c + Q)
                g.tensor_tensor(h_rows[:, t, 0:D], h_rows[:, t, 0:D], score[:, t].unsqueeze(2).broadcast_to([P, Q, D]), ALU.mult
                                ).then_inc(hs_pool, 1)
            pool.wait_ge(zero_st, 16 * ZERO_LOADS)
            pool.wait_ge(pos_rdy, 1)
            pool.wait_ge(k_ids, 2)
            for t in range(NT):
                if t < Q * POOL_QUADS:
                    pool.wait_ge(hs_pool, t // Q + 1)
                else:
                    pool.wait_ge(hs_rdy, t - Q * POOL_QUADS + 1)
                g.indirect_dma_start(out=x_slots, out_offset=bass.IndirectOffsetOnAxis(ap=pos[:, t:t + 1], axis=0),
                                     in_=h_rows[:, t, :], in_offset=None).then_inc(scat, 16)
            for g_no in range(NG):
                pool.wait_ge(home_rdy, g_no + 1)
                pool.wait_ge(yg_rdy, g_no + 1)
                for n in range(Q * g_no, Q * g_no + Q):
                    g.indirect_dma_start(out=y_rows, out_offset=bass.IndirectOffsetOnAxis(ap=home[:, n:n + 1], axis=0),
                                         in_=yg[:, n, :], in_offset=None).then_inc(back, 16)
            for c in range(POOL_FINAL):
                pool.wait_ge(ld_y[c], 16)
                pool.wait_ge(y_free, c + 2)
                r = xres[:, Q * c:Q * c + Q, :]
                g.tensor_tensor(r, r, h_rows[:, Q * c:Q * c + Q, 0:D], ALU.add).then_inc(fin_pool, 1)

        @block.scalar
        def _(act):
            a = nc.scalar
            act.dma_start(m_col[:], m.unsqueeze(1).broadcast_to([HEADS, HD])).then_inc(ld_m, 16)
            for dst, src in ((w_qkv[:, 0:D], Wq), (w_qkv[:, D:2 * D], Wk), (w_qkv[:, 2 * D:QKV], Wv)):
                act.dma_start(dst, src).then_inc(ld_wa, 16)
            act.wait_ge(ld_m, 16)
            act.wait_ge(k_col, 1)
            a.activation(m_tmp[:, 0:1], m_col[:], ACT.Exp, bias=zero_col[:], scale=-1.0).then_inc(ach, 1)
            act.wait_ge(m_step, 1)
            a.activation(m_tmp[:, 3:4], m_tmp[:, 2:3], ACT.Exp, bias=zero_col[:],
                         scale=-float(np.log(S))).then_inc(ach, 1)

            def std(dst, mv, var, done, c):
                t = slice(Q * c, Q * c + Q)
                act.wait_ge(var, c + 1)
                a.activation(dst[:, t], mv[:, t, 1], ACT.Sqrt, bias=eps_col[:], scale=1.0).then_inc(done, 1)

            def norm_h(c):
                act.wait_ge(rstd2, c + 1)
                for t in tiles(c):
                    last = a.activation(h_rows[:, t, 0:D], xres[:, t, :], ACT.Identity, bias=nm2[:, t:t + 1],
                                        scale=rs2[:, t:t + 1])
                last.then_inc(h_rdy, 1)

            def xT_copy(c):
                act.wait_ge(xT_mm, turn_no["x", c])
                if c >= 2:
                    act.wait_ge(qkv_mm, 2 * (c - 1))
                a.copy(xT[:, c % 2], ps_xT[:]).then_inc(xT_sb, 1)

            def hT_hi(c):
                act.wait_ge(xT_mm, turn_no["h", c])
                if c >= 2:
                    act.wait_ge(hT_rdy, c - 1)
                a.copy(hT_raw[:, c % 2], ps_xT[:]).then_inc(xT_sb, 1)
                act.wait_ge(xT_sb, turn_no["h", c])
                a.copy(hT[:, 0, 512 * c:512 * c + 512], hT_raw[:, c % 2]).then_inc(hT_hi_rdy, 1)

            def square(c):
                act.wait_ge(qkv_sb, 2 * (c + 1))
                if c >= 1:
                    act.wait_ge(ss_done, c)
                a.activation(sq[:], qkv[:, c % QRING, :, 0:2 * D], ACT.Square).then_inc(sq_done, 1)

            def head_norms(c):
                act.wait_ge(ssum, c + 1)
                if c >= 2:
                    act.wait_ge(q_rdy, c - 1)
                a.activation(rn[:, c % 2], ss[:, c % 2], ACT.Sqrt).then_inc(nrm, 1)

            def qT_copy(c):
                act.wait_ge(qT_mm, c + 1)
                if c >= RING:
                    act.wait_ge(y_mm, c - RING + 1)
                a.copy(qT[:, c % RING], ps_qy[:]).then_inc(qT_sb, 1)

            def wb_copy(b):
                act.wait_ge(wb_mm, b + 1)
                if b >= 2:
                    act.wait_ge(y_mm, QB * (b - 1))
                a.copy(wb[:, b % 2], ps_vk[:, D:2 * D]).then_inc(wb_rdy, 1)

            def split_hi(n):
                act.wait_ge(ld_we[n], 16)
                a.copy(w_gu[:, 0, n * EC:n * EC + EC, :], w_raw[:, n % 2]).then_inc(we_hi, 1)

            def weights_hi(n):
                act.wait_ge(su_mm, n + 1)
                dst = (sgT, suT, sdT, rwT)[n][:, 0]
                a.copy(dst, setup_bank[:, 0:dst.shape[1]]).then_inc(su_cp, 1)

            def silu_shared(c, k):
                n = c * KC + k
                act.wait_ge(s_gu_mm, n + 1)
                a.activation(sg_act[:, k % 2], pair[:, 2 * (k % 2)], ACT.Silu).then_inc(s_silu, 1)

            def hi_shared(c, k):
                act.wait_ge(s_act_rdy, c * KC + k + 1)
                if not (isinstance(c, int) and c == 0 and k < 2):
                    act.wait_ge(s_dn_mm, c * KC + k - 1)
                a.copy(s_spl[:, k % 2, 0], s_act[:, k % 2]).then_inc(s_hi, 1)

            act.wait_ge(wc_mm, 1)
            a.copy(w_c[:], pair[:, 0, 0:QKV]).then_inc(wc_rdy, 1)
            xT_copy(0)
            std(rs1, mv1, var1, std1, 0)
            for s in range(STEPS):
                if live(s + 1):
                    std(rs1, mv1, var1, std1, s + 1)
                if s in SPLIT_STEPS:
                    split_hi(SPLIT_STEPS.index(s))
                if s == STEPS - 1:
                    silu_shared(0, 0)
                if live(s - 4):
                    hT_hi(s - 4)
                if 1 <= s < 5:
                    weights_hi(s - 1)
                if live(s):
                    square(s)
                if live(s - 1):
                    qT_copy(s - 1)
                if live(s - 3):
                    std(rs2, mv2, var2, std2, s - 3)
                if live(s + 1):
                    xT_copy(s + 1)
                if live(s):
                    head_norms(s)
                if live(s - 3):
                    norm_h(s - 3)
                if live(s - 1) and (s - 1) % 2:
                    wb_copy((s - 1) // 2)

            silu_shared(0, 1)
            hi_shared(0, 0)
            silu_shared(0, 2)
            hi_shared(0, 1)
            act.wait_ge(top_rdy, 1)
            a.activation(score[:], top[:], ACT.Sigmoid).then_inc(score_rdy, 1)
            act.wait_ge(score_rdy, 1)
            act.wait_ge(xT_mm, 2 * NQ)
            for t in range(Q * POOL_QUADS, NT):
                a.activation(h_rows[:, t, 0:D], h_rows[:, t, 0:D], ACT.Copy, scale=score[:, t:t + 1]).then_inc(hs_rdy, 1)
            silu_shared(0, 3)
            hi_shared(0, 2)

            def yT_copy(c):
                act.wait_ge(s_dn_mm, (c + 1) * KC)
                a.copy(yT[:], ps_yT[:]).then_inc(yT_sb, 1)

            def shared(lo, hi):
                if lo > 0:
                    hi_shared(lo, 0)
                    for k in range(2, KC):
                        silu_shared(lo, k)
                        hi_shared(lo, k - 1)
                with act.Fori(lo + 1, hi) as c:
                    silu_shared(c, 0)
                    hi_shared(c - 1, KC - 1)
                    silu_shared(c, 1)
                    hi_shared(c, 0)
                    yT_copy(c - 1)
                    for k in range(2, KC):
                        silu_shared(c, k)
                        hi_shared(c, k - 1)
                hi_shared(hi - 1, KC - 1)
                if hi < NQ:
                    experts(0, 0, (0,))
                yT_copy(hi - 1)

            def experts(i, par, stages=(3, 2, 1, 0)):
                g = i * 2 + par
                if 0 in stages:
                    act.wait_ge(gT_mm, g + 1)
                    a.copy(xgT[:, par, 0], ps_gT[:]).then_inc(gT_hi, 1)
                if 1 in stages:
                    act.wait_ge(e_gu_mm, g)
                    a.activation(eg_act[:, (par - 1) % 2], gate_up_banks((par - 1) % 2)[:, :, 0:F],
                                 ACT.Silu).then_inc(e_silu, 1)
                if 3 in stages:
                    act.wait_ge(e_dn_mm, g - 2)
                    a.copy(yg[:, bass.ds((g - 3) * Q, Q), :], ps_yg[:].rearrange("p (j d) -> p j d", d=D)
                           ).then_inc(yg_rdy, 1)

            shared(0, C1)
            over_groups(experts, act, lambda k: silu_shared(C1, k))
            shared(C1, NQ)

        @block.vector
        def _(dve):
            v = nc.vector
            links = [0]

            def link(ins):
                links[0] += 1
                ins.then_inc(dch, 1)
                dve.wait_ge(dch, links[0])

            def stats(c, st, mv, done):
                for t in tiles(c):
                    last = v.bn_stats(st[:, t, :], xres[:, t, :])
                link(last)
                for t in tiles(c):
                    last = v.bn_aggr(mv[:, t, :], st[:, t, :])
                last.then_inc(done, 1)

            def x_stats(c):
                dve.wait_ge(ld_x[c], 16)
                stats(c, st1, mv1, var1)

            def x_scales(c):
                t = slice(Q * c, Q * c + Q)
                dve.wait_ge(std1, c + 1)
                v.reciprocal(rs1[:, t], rs1[:, t]).then_inc(rstd1, 1)

            def h_scales(c):
                t = slice(Q * c, Q * c + Q)
                dve.wait_ge(std2, c + 1)
                link(v.reciprocal(rs2[:, t], rs2[:, t]))
                v.scalar_tensor_tensor(out=nm2[:, t], in0=mv2[:, t, 0], scalar=-1.0, in1=rs2[:, t], op0=ALU.mult,
                                       op1=ALU.mult).then_inc(rstd2, 1)

            def take_qkv(c):
                if c == 0:
                    dve.wait_ge(ld_b, 16 * 3)
                dve.wait_ge(rstd1, c + 1)
                if c >= QRING:
                    dve.wait_ge(qT_mm, c - QRING + 1)
                    dve.wait_ge(vk_mm, c - QRING + 1)
                for j, t in enumerate(tiles(c)):
                    if j % 2 == 0:
                        dve.wait_ge(qkv_mm, 2 * c + j // 2 + 1)
                    last = v.scalar_tensor_tensor(out=qkv[:, c % QRING, j, :], in0=pair[:, j, 0:QKV],
                                                  scalar=rs1[:, t:t + 1], in1=b_qkv[:], op0=ALU.mult, op1=ALU.add)
                    if j % 2:
                        last.then_inc(qkv_sb, 1)

            def head_sums(c):
                dve.wait_ge(sq_done, c + 1)
                if c >= 2:
                    dve.wait_ge(nrm, c - 1)
                v.tensor_reduce(ss[:, c % 2], sq[:].rearrange("p j (n d) -> p j n d", d=HD), AX.X, ALU.add
                                ).then_inc(ss_done, 1)
                dve.wait_ge(ss_done, c + 1)
                v.tensor_scalar(ss[:, c % 2], ss[:, c % 2], 1e-24, None, ALU.max).then_inc(ssum, 1)

            def inv_norms(c):
                dve.wait_ge(nrm, c + 1)
                v.reciprocal(rn[:, c % 2], rn[:, c % 2]).then_inc(rn_rdy, 1)

            def mask_vk(b):
                dve.wait_ge(vk_mm, QB * (b + 1))
                if b >= 2:
                    dve.wait_ge(wb_mm, b - 1)
                v.tensor_tensor(vkm[:, b % 2], ps_vk[:, 0:D], head_mask[:], ALU.mult).then_inc(vkm_rdy, 1)

            def add_attn(c):
                dve.wait_ge(y_mm, c + 1)
                dve.wait_ge(bo_add, c + 1)
                r = xres[:, Q * c:Q * c + Q, :]
                v.tensor_tensor(r, ps_qy[:].rearrange("p (j d) -> p j d", d=D), r, ALU.add).then_inc(x1_rdy, 1)
                dve.wait_ge(x1_rdy, c + 1)
                stats(c, st2, mv2, var2)

            def weights_lo(n):
                dve.wait_ge(su_cp, n + 1)
                w = (sgT, suT, sdT, rwT)[n]
                v.tensor_tensor(w[:, 1], setup_bank[:, 0:w.shape[2]], w[:, 0].bitcast(F32), ALU.subtract
                                ).then_inc(su_lo, 1)

            def act_shared(c, k):
                dve.wait_ge(s_silu, c * KC + k + 1)
                if not (isinstance(c, int) and c == 0 and k < 2):
                    dve.wait_ge(s_spl_rdy, c * KC + k - 1)
                v.tensor_tensor(s_act[:, k % 2], pair[:, 2 * (k % 2) + 1], sg_act[:, k % 2], ALU.mult
                                ).then_inc(s_act_rdy, 1)

            def lo_shared(c, k):
                dve.wait_ge(s_hi, c * KC + k + 1)
                v.tensor_tensor(s_spl[:, k % 2, 1], s_act[:, k % 2], s_spl[:, k % 2, 0].bitcast(F32), ALU.subtract
                                ).then_inc(s_spl_rdy, 1)

            dve.wait_ge(k_id, 1)
            v.tensor_scalar(center[:], ident[:], -1.0 / D, None, ALU.add).then_inc(center_rdy, 1)
            dve.wait_ge(ach, 1)
            link(v.tensor_scalar(m_tmp[:, 1:2], m_tmp[:, 0:1], 1.0, None, ALU.add))
            v.reciprocal(m_tmp[:, 2:3], m_tmp[:, 1:2]).then_inc(m_step, 1)
            dve.wait_ge(ach, 2)
            dve.wait_ge(k_pool, 2)
            link(v.tensor_scalar(head_mask[:], head_mask[:], m_tmp[:, 3:4], None, ALU.mult))
            x_stats(0)
            x_scales(0)
            x_stats(1)
            for s in range(STEPS):
                if live(s):
                    take_qkv(s)
                if live(s - 3):
                    add_attn(s - 3)
                if live(s - 1) and (s - 1) % 2:
                    mask_vk((s - 1) // 2)
                if 1 <= s < 5:
                    weights_lo(s - 1)
                if live(s):
                    head_sums(s)
                if live(s + 1):
                    x_scales(s + 1)
                if live(s - 3):
                    h_scales(s - 3)
                if live(s + 2):
                    x_stats(s + 2)
                if live(s):
                    inv_norms(s)
            v.engine_nop().then_inc(y_free, 1)
            act_shared(0, 0)
            act_shared(0, 1)
            lo_shared(0, 0)

            dve.wait_ge(log_mm, NQ)
            dve.wait_ge(k_pool, 2)
            logits = ps_log[:].rearrange("p (t e) -> p t e", e=E)
            v.tensor_reduce(top[:], logits, AX.X, ALU.max).then_inc(top_rdy, 1)
            dve.wait_ge(top_rdy, 1)
            link(v.tensor_tensor(key[:], logits, top[:].unsqueeze(2).broadcast_to([P, NT, E]), ALU.is_equal))
            link(v.tensor_tensor(key[:], key[:], rank_key[:], ALU.mult))
            link(v.tensor_reduce(ktop[:], key[:], AX.X, ALU.max))
            link(v.tensor_tensor(hot[:].rearrange("p e t -> p t e"), key[:],
                                 ktop[:].unsqueeze(2).broadcast_to([P, NT, E]), ALU.is_equal))
            v.tensor_reduce(cnt[:], hot[:], AX.X, ALU.add).then_inc(cnt_rdy, 1)
            link(v.tensor_tensor_scan(run[:].rearrange("p e t -> p (e t)"), run_mask[:].rearrange("p e t -> p (e t)"),
                                      hot[:].rearrange("p e t -> p (e t)"), 0.0, ALU.mult, ALU.add))
            act_shared(0, 2)
            lo_shared(0, 1)
            dve.wait_ge(cnt_mm, 1)
            link(v.tensor_scalar(tot_i[:], ps_vk[:, 32:32 + E], float(P - 1), None, ALU.add))
            link(v.tensor_scalar(til_i[:], tot_i[:], P.bit_length() - 1, None, ALU.logical_shift_right))
            link(v.tensor_copy(til[:], til_i[:]))
            link(v.tensor_tensor_scan(til_end[:], ones[:, 0:E], til[:], 0.0, ALU.mult, ALU.add))
            link(v.tensor_tensor(base[:], til_end[:], til[:], ALU.subtract))
            link(v.tensor_scalar(base[:], base[:], float(P), -1.0, ALU.mult, ALU.add))
            link(v.tensor_tensor(base[:], ps_vk[:, 0:E], base[:], ALU.add))
            link(v.tensor_tensor(run[:], run[:], base[:].unsqueeze(2).broadcast_to([P, E, NT]), ALU.add))
            link(v.tensor_tensor(run[:], run[:], hot[:], ALU.mult))
            link(v.tensor_reduce(pos_f[:], run[:].rearrange("p e t -> p t e"), AX.X, ALU.add))
            v.tensor_copy(pos[:], pos_f[:]).then_inc(pos_rdy, 1)
            act_shared(0, 3)
            lo_shared(0, 2)
            link(v.tensor_tensor(past[:], til_end[0:1, :].unsqueeze(1).broadcast_to([1, SLOT_TILES, E]), tile_no[:],
                                 ALU.is_le))
            link(v.tensor_reduce(eid_f[:], past[:], AX.X, ALU.add))
            v.tensor_scalar(eid[:, 3:NG + 3, 0], eid_f[:].rearrange("o (g j) -> o g j", j=Q), float(E - 1), float(D), ALU.min,
                            ALU.mult).then_inc(eid_rdy, 1)
            v.tensor_scalar(eid[:, 1:NG + 1, 1], eid_f[:].rearrange("o (g j) -> o g j", j=Q), float(E - 1), float(D), ALU.min,
                            ALU.mult).then_inc(eid_rdy, 1)

            def add_shared(c):
                dve.wait_ge(yT_mm, c + 1)
                r = xres[:, bass.ds(c * Q, Q), :]
                v.tensor_tensor(r, ps_y[:].rearrange("p (j d) -> p j d", d=D), r, ALU.add).then_inc(y_free, 1)

            def shared(lo, hi):
                if lo > 0:
                    lo_shared(lo, 0)
                    for k in range(2, KC):
                        act_shared(lo, k)
                        lo_shared(lo, k - 1)
                with dve.Fori(lo + 1, hi) as c:
                    act_shared(c, 0)
                    lo_shared(c - 1, KC - 1)
                    act_shared(c, 1)
                    lo_shared(c, 0)
                    act_shared(c, 2)
                    lo_shared(c, 1)
                    add_shared(c - 1)
                    act_shared(c, 3)
                    lo_shared(c, 2)
                lo_shared(hi - 1, KC - 1)
                if hi < NQ:
                    dve.wait_ge(k_ids, 2)
                    experts(0, 0, (0,))
                add_shared(hi - 1)

            def experts(i, par, stages=(3, 2, 1, 0)):
                g = i * 2 + par
                if 0 in stages:
                    dve.wait_ge(xg_ld[par], (i + 1) * 16)
                    here = bass.ds(g * Q, Q)
                    v.scalar_tensor_tensor(out=away[:, here], in0=xg[:, par, :, D], scalar=0.0, in1=free_row[:, here],
                                           op0=ALU.is_equal, op1=ALU.mult).then_inc(away_rdy, 1)
                    dve.wait_ge(away_rdy, g + 1)
                    v.tensor_tensor(home[:, here], xg[:, par, :, D], away[:, here], ALU.add).then_inc(home_rdy, 1)
                    dve.wait_ge(gT_hi, g + 1)
                    v.tensor_tensor(xgT[:, par, 1], ps_gT[:], xgT[:, par, 0].bitcast(F32), ALU.subtract
                                    ).then_inc(gT_sb, 1)
                if 1 in stages:
                    dve.wait_ge(e_silu, g)
                    v.tensor_tensor(e_act[:, (par - 1) % 2], gate_up_banks((par - 1) % 2)[:, :, F:F2],
                                    eg_act[:, (par - 1) % 2], ALU.mult).then_inc(e_act_rdy, 1)
                if 2 in stages:
                    dve.wait_ge(aT_mm, g - 1)
                    v.tensor_copy(e_actT[:, par], ps_aT[:]).then_inc(aT_sb, 1)

            shared(0, C1)
            over_groups(experts, dve, lambda k: act_shared(C1, k))
            shared(C1, NQ)
            dve.wait_ge(y_free, NQ + 1)
            for c in range(POOL_FINAL, NQ):
                dve.wait_ge(ld_y[c], 16)
                r = xres[:, Q * c:Q * c + Q, :]
                v.tensor_tensor(r, r, h_rows[:, Q * c:Q * c + Q, 0:D], ALU.add).then_inc(fin, 1)

        @block.tensor
        def _(pe):
            te = nc.tensor
            pe.wait_ge(k_id, 1)

            def center_weights():
                pe.wait_ge(center_rdy, 1)
                pe.wait_ge(ld_wa, 16 * 3)
                te.matmul(pair[:, 0, 0:QKV], center[:], w_qkv[:], start=True, stop=True).then_inc(wc_mm, 1)

            def turn(src, kind, c):
                n = turn_no[kind, c]
                if kind == "x":
                    pe.wait_ge(ld_x[c], 16)
                else:
                    pe.wait_ge(h_rdy, c + 1)
                if n > 1:
                    pe.wait_ge(xT_sb, n - 1)
                for j, t in enumerate(tiles(c)):
                    last = te.transpose(ps_xT[:, P * j:P * j + P], src[:, t, 0:D], ident[:])
                last.then_inc(xT_mm, 1)

            def project(c):
                if c == 0:
                    pe.wait_ge(wc_rdy, 1)
                pe.wait_ge(xT_sb, turn_no["x", c])
                for j in range(Q):
                    if j % 2 == 0 and c >= 1:
                        pe.wait_ge(qkv_sb, 2 * (c - 1) + j // 2 + 1)
                    last = te.matmul(pair[:, j, 0:QKV], xT[:, c % 2, P * j:P * j + P], w_c[:], start=True, stop=True)
                    if j % 2:
                        last.then_inc(qkv_mm, 1)

            def v_by_k(c):
                b, h = divmod(c, QB)
                if h == 0 and b >= 1:
                    pe.wait_ge(wb_rdy, b)
                pe.wait_ge(v_rdy, c + 1)
                for j in range(Q):
                    last = te.matmul(ps_vk[:, 0:D], qkv[:, c % QRING, j, 2 * D:QKV], qkv[:, c % QRING, j, D:2 * D],
                                     start=(h == 0 and j == 0), stop=(h == QB - 1 and j == Q - 1))
                last.then_inc(vk_mm, 1)

            def fold_wo(b):
                if b == 0:
                    pe.wait_ge(ld_wo, 16 * 2)
                pe.wait_ge(vkm_rdy, b + 1)
                te.matmul(ps_vk[:, D:2 * D], vkm[:, b % 2], w_o[:], start=True, stop=True).then_inc(wb_mm, 1)

            def turn_q(c):
                pe.wait_ge(q_rdy, c + 1)
                if c >= 2:
                    pe.wait_ge(x1_rdy, c - 1)
                if c >= 1:
                    pe.wait_ge(qT_sb, c)
                for j in range(Q):
                    last = te.transpose(ps_qy[:, P * j:P * j + P], qkv[:, c % QRING, j, 0:D], ident[:])
                last.then_inc(qT_mm, 1)

            def attend(c):
                pe.wait_ge(qT_sb, min(c + 2, NQ))
                pe.wait_ge(wb_rdy, c // QB + 1)
                if c >= 1:
                    pe.wait_ge(x1_rdy, c)
                for j in range(Q):
                    last = te.matmul(ps_qy[:, P * j:P * j + P], qT[:, c % RING, P * j:P * j + P], wb[:, c // QB % 2],
                                     start=True, stop=True)
                last.then_inc(y_mm, 1)

            def split_product(out, lhs, rhs):
                te.matmul(out, lhs[:, 0], rhs[:, 0], start=True, stop=False)
                te.matmul(out, lhs[:, 0], rhs[:, 1], start=False, stop=False)
                return te.matmul(out, lhs[:, 1], rhs[:, 0], start=False, stop=True)

            def route(c):
                pe.wait_ge(hT_rdy, c + 1)
                for t in tiles(c):
                    last = split_product(ps_log[:, E * t:E * t + E], hT[:, :, P * t:P * t + P], rwT)
                last.then_inc(log_mm, 1)

            def turn_weights(n):
                if n == 0:
                    pe.wait_ge(ld_ws, 16 * 4)
                else:
                    pe.wait_ge(su_lo, n)
                if n == 3:
                    last = te.transpose(setup_bank[:, 0:E], rw_in[:], ident[0:E, 0:E])
                else:
                    for k in range(KC):
                        src = (sg_in[:, k, :], su_in[:, k, :], sd_in[:, P * k:P * k + P])[n]
                        last = te.transpose(setup_bank[:, P * k:P * k + P], src, ident[:])
                last.then_inc(su_mm, 1)

            def gate_up_shared(c, k):
                n = c * KC + k
                if not (isinstance(c, int) and n < 2):
                    pe.wait_ge(s_act_rdy, n - 1)
                h = hT[:, :, bass.ds(c * 512, 512)]
                split_product(pair[:, 2 * (k % 2)], sgT[:, :, P * k:P * k + P], h)
                split_product(pair[:, 2 * (k % 2) + 1], suT[:, :, P * k:P * k + P], h).then_inc(s_gu_mm, 1)

            def down_shared(c, k):
                pe.wait_ge(s_spl_rdy, c * KC + k + 1)
                if k == 0 and not (isinstance(c, int) and c == 0):
                    pe.wait_ge(yT_sb, c)
                w, h = sdT[:, :, D * k:D * k + D], s_spl[:, k % 2]
                te.matmul(ps_yT[:], w[:, 0], h[:, 0], start=(k == 0), stop=False)
                te.matmul(ps_yT[:], w[:, 1], h[:, 0], start=False, stop=False)
                te.matmul(ps_yT[:], w[:, 0], h[:, 1], start=False, stop=(k == KC - 1)).then_inc(s_dn_mm, 1)

            turn(xres, "x", 0)
            center_weights()
            for s in range(STEPS):
                if live(s):
                    project(s)
                if live(s - 4):
                    turn(h_rows, "h", s - 4)
                if live(s - 3):
                    attend(s - 3)
                if s == STEPS - 2:
                    pe.wait_ge(qkv_sb, 2 * NQ)
                    gate_up_shared(0, 0)
                if s == STEPS - 1:
                    gate_up_shared(0, 1)
                    gate_up_shared(0, 2)
                if live(s - 1):
                    v_by_k(s - 1)
                    turn_q(s - 1)
                if live(s + 1):
                    turn(xres, "x", s + 1)
                if s < 4:
                    turn_weights(s)
                if live(s - 4):
                    if s == 4:
                        pe.wait_ge(su_lo, 4)
                    route(s - 4)
                if live(s - 1):
                    if (s - 1) % 2:
                        fold_wo((s - 1) // 2)

            down_shared(0, 0)
            pe.wait_ge(cnt_rdy, 1)
            te.matmul(ps_vk[:, 0:E], before[:], cnt[:], start=True, stop=True)
            te.matmul(ps_vk[:, 32:32 + E], ones[:], cnt[:], start=True, stop=True).then_inc(cnt_mm, 1)
            gate_up_shared(0, 3)
            down_shared(0, 1)

            def turn_y(c, first=False):
                pe.wait_ge(yT_sb, c + 1)
                pe.wait_ge(y_free, c + 1)
                for j in range(Q):
                    last = te.transpose(ps_y[:, P * j:P * j + P], yT[:, P * j:P * j + P], ident[:])
                last.then_inc(yT_mm, 1)

            def shared(lo, hi):
                if lo > 0:
                    for k in range(2, KC):
                        gate_up_shared(lo, k)
                        down_shared(lo, k - 2)
                with pe.Fori(lo + 1, hi) as c:
                    gate_up_shared(c, 0)
                    down_shared(c - 1, KC - 2)
                    gate_up_shared(c, 1)
                    down_shared(c - 1, KC - 1)
                    gate_up_shared(c, 2)
                    turn_y(c - 1)
                    down_shared(c, 0)
                    gate_up_shared(c, 3)
                    down_shared(c, 1)
                if hi < NQ:
                    experts(0, 0, (0,))
                down_shared(hi - 1, KC - 2)
                down_shared(hi - 1, KC - 1)
                turn_y(hi - 1)

            def columns(g, which):
                _, vals = nc.values_load_multi_w_load_instructions(
                    eid_flat[0:1, bass.ds((g * 2 + which) * Q, Q)], engines=(mybir.EngineType.PE,), min_val=0,
                    max_val=(E - 1) * D,
                    skip_runtime_bounds_check_because="VectorE made them as D * min(a count of experts, E - 1)")
                return vals

            eid_flat = eid[:].rearrange("o g s j -> o (g s j)")
            gu_cols = w_gu[:].rearrange("p s e c -> p s (e c)")
            dn_cols = w_dn[:].rearrange("p e c -> p (e c)")

            def experts(i, par, stages=(3, 2, 1, 0)):
                g = i * 2 + par
                if 0 in stages:
                    pe.wait_ge(xg_ld[par], (i + 1) * 16)
                    if not (isinstance(g, int) and g == 0):
                        pe.wait_ge(gT_sb, g)
                    for j in range(Q):
                        mm = te.transpose(ps_gT[:, P * j:P * j + P], xg[:, par, j, 0:D], ident[:])
                    mm.then_inc(gT_mm, 1)
                if 1 in stages:
                    cols = columns(g, 1)
                    pe.wait_ge(gT_sb, g)
                    for j in range(Q):
                        mm = split_product(gate_up_banks((par - 1) % 2)[:, j, :],
                                           xgT[:, (par - 1) % 2, :, P * j:P * j + P],
                                           gu_cols[:, :, bass.ds(cols[j] * 2, F2)])
                    mm.then_inc(e_gu_mm, 1)
                if 3 in stages:
                    cols = columns(g, 0)
                    pe.wait_ge(aT_sb, g - 2)
                    if not (isinstance(g, int) and g == 3):
                        pe.wait_ge(yg_rdy, g - 3)
                    for j in range(Q):
                        mm = te.matmul(ps_yg[:, P * j:P * j + P], e_actT[:, (par - 3) % 2, P * j:P * j + P],
                                       dn_cols[:, bass.ds(cols[j], D)], start=True, stop=True)
                    mm.then_inc(e_dn_mm, 1)
                if 2 in stages:
                    pe.wait_ge(e_act_rdy, g - 1)
                    if not (isinstance(g, int) and g == 2):
                        pe.wait_ge(aT_sb, g - 2)
                    for j in range(Q):
                        mm = te.transpose(ps_aT[:, P * j:P * j + P], e_act[:, par, j, :], ident[:])
                    mm.then_inc(aT_mm, 1)

            shared(0, C1)
            pe.wait_ge(eid_rdy, 2)
            pe.wait_ge(we_lo, E // EC)
            pe.wait_ge(ld_wd, 16)
            over_groups(experts, pe, lambda k: gate_up_shared(C1, k))
            shared(C1, NQ)


_INS = ["L0_attn_x", "L0_attn_Wq", "L0_attn_bq", "L0_attn_Wk", "L0_attn_bk", "L0_attn_Wv", "L0_attn_bv", "L0_attn_Wo",
        "L0_attn_bo", "L0_attn_m", "L0_ffn_router_w", "L0_ffn_gate_up_proj", "L0_ffn_down_proj",
        "L0_ffn_shared_gate_w", "L0_ffn_shared_up_w", "L0_ffn_shared_down_w"]


def kernel(**inputs):
    import concourse.bacc as bacc
    from concourse.bass_utils import run_bass_kernel_spmd

    nc = bacc.Bacc("TRN2", target_bir_lowering=False, num_devices=1)
    arrays = {name: np.ascontiguousarray(inputs[name]) for name in _INS}
    args = [nc.dram_tensor(name, a.shape, F32, kind="ExternalInput").ap() for name, a in arrays.items()]
    out = nc.dram_tensor("out", arrays["L0_attn_x"].shape, F32, kind="ExternalOutput").ap()
    build_block(nc, *args, out)
    return run_bass_kernel_spmd(nc, [arrays], core_ids=[0]).results[0]["out"]
```

```python
from contextlib import ExitStack

import numpy as np

import concourse.bass as bass
from concourse import mybir

ALU = mybir.AluOpType
ACT = mybir.ActivationFunctionType
AX = mybir.AxisListType
F32 = mybir.dt.float32
F32R = mybir.dt.float32r
I32 = mybir.dt.int32

P = 128


def build_block(nc, x, Wq, bq, Wk, bk, Wv, bv, Wo, bo, m, router_w, gate_up, down, shared_gate, shared_up,
                shared_down, out):
    B, S, D = x.shape
    HEADS = m.shape[0]
    HD = D // HEADS
    E, _, F2 = gate_up.shape
    F = F2 // 2
    SF = shared_gate.shape[0]
    T = B * S
    NT = T // P
    TB = S // P
    Q = 4
    NQ = NT // Q
    QB = TB // Q
    KC = SF // P
    NG = -(-(NT + E - 1) // Q)
    SLOT_TILES = NG * Q
    SLOTS = SLOT_TILES * P
    QKV = 3 * D
    W = D + 1
    QRING = 2
    RING = 3
    EPS = 1e-5
    EC = 4
    C1 = 5
    ZERO_LOADS = 8
    ZW = SLOT_TILES * W // ZERO_LOADS
    POOL_FINAL = NQ - 4
    POOL_QUADS = 5
    EARLY = NQ - 2
    assert D == P and F == P and QB == 2 and NG == 12 and KC == 4

    x_slots = nc.dram_tensor("x_slots", (SLOTS, W), F32, kind="Internal").ap()
    y_rows = nc.dram_tensor("y_rows", (1 + T + SLOTS, D), F32, kind="Internal").ap()
    x_rows = x.rearrange("b (j p) d -> p (b j) d", p=P)
    out_rows = out.rearrange("b (j p) d -> p (b j) d", p=P)

    with ExitStack() as ctx:
        def sb(name, shape, dt=F32):
            return ctx.enter_context(nc.sbuf_tensor(name, shape, dt))

        def sem(name):
            return ctx.enter_context(nc.semaphore(name))

        xres = sb("xres", [P, NT, D])
        h_rows = sb("h_rows", [P, NT, W])
        hT = sb("hT", [P, 2, T], F32R)
        st1 = sb("st1", [P, NT, 6])
        mv1 = sb("mv1", [P, NT, 2])
        rs1 = sb("rs1", [P, NT])
        nm2 = sb("nm2", [P, NT])
        st2 = sb("st2", [P, NT, 6])
        mv2 = sb("mv2", [P, NT, 2])
        rs2 = sb("rs2", [P, NT])
        w_o = sb("w_o", [P, D])
        ident = sb("ident", [P, P])
        before = sb("before", [P, P])
        ones = sb("ones", [P, P])
        eps_col = sb("eps_col", [P, 1])
        zero_col = sb("zero_col", [P, 1])
        rwT = sb("rwT", [P, 2, E], F32R)
        sgT = sb("sgT", [P, 2, SF], F32R)
        suT = sb("suT", [P, 2, SF], F32R)
        sdT = sb("sdT", [P, 2, KC * D], F32R)
        w_gu = sb("w_gu", [P, 2, E, F2], F32R)
        w_dn = sb("w_dn", [P, E, D])
        sg_act = sb("sg_act", [P, 2, 512])
        s_act = sb("s_act", [P, 2, 512])
        s_spl = sb("s_spl", [P, 2, 2, 512], F32R)
        yT = sb("yT", [P, 512])
        top = sb("top", [P, NT])
        score = sb("score", [P, NT])
        cnt = sb("cnt", [P, E])
        cnt_part = sb("cnt_part", [P, 2, E])
        tot_i = sb("tot_i", [P, E], I32)
        til_i = sb("til_i", [P, E], I32)
        til = sb("til", [P, E])
        til_end = sb("til_end", [P, E])
        base = sb("base", [P, 2, E])
        ahead = sb("ahead", [P, NT])
        first = sb("first", [P, NT])
        pos = sb("pos", [P, NT], I32)
        eid_f = sb("eid_f", [1, SLOT_TILES])
        eid = sb("eid", [1, NG + 3, 2, Q], I32)
        rank_key = sb("rank_key", [P, NT, E])
        free_row = sb("free_row", [P, SLOT_TILES])
        PARTS = (slice(0, Q * EARLY), slice(Q * EARLY, NT))
        sizes = [part.stop - part.start for part in PARTS]
        run_mask = [sb(f"run_mask{i}", [P, E, n]) for i, n in enumerate(sizes)]
        ktop = [sb(f"ktop{i}", [P, n]) for i, n in enumerate(sizes)]
        hot = [sb(f"hot{i}", [P, E, n]) for i, n in enumerate(sizes)]
        run = [sb(f"run{i}", [P, E, n]) for i, n in enumerate(sizes)]
        key = [r[:].rearrange("p e t -> p (e t)").rearrange("p (t e) -> p t e", e=E) for r in run]
        tile_no = sb("tile_no", [1, SLOT_TILES, E])

        with ExitStack() as attention:
            def sb_a(name, shape, dt=F32):
                return attention.enter_context(nc.sbuf_tensor(name, shape, dt))

            w_raw = sb_a("w_raw", [P, 2, EC, F2])
            qkv = sb_a("qkv", [P, QRING, Q, QKV])
            sq = sb_a("sq", [P, Q, 2 * D])
            xT = sb_a("xT", [P, 2, Q * P])
            hT_raw = sb_a("hT_raw", [P, 2, Q * P])
            qT = sb_a("qT", [P, RING, Q * P])
            ss = sb_a("ss", [P, 2, Q, 2 * HEADS])
            rn = sb_a("rn", [P, 2, Q, 2 * HEADS])
            vkm = sb_a("vkm", [P, 2, D])
            wb = sb_a("wb", [P, 2, D])
            w_qkv = sb_a("w_qkv", [P, QKV])
            b_qkv = sb_a("b_qkv", [P, QKV])
            center = sb_a("center", [P, P])
            w_c = sb_a("w_c", [P, QKV])
            b_o = sb_a("b_o", [P, D])
            m_col = sb_a("m_col", [P, 1])
            m_tmp = sb_a("m_tmp", [P, 4])
            head_mask = sb_a("head_mask", [P, D])
            rw_in = sb_a("rw_in", [E, D])
            sg_in = sb_a("sg_in", [P, KC, D])
            su_in = sb_a("su_in", [P, KC, D])
            sd_in = sb_a("sd_in", [P, SF])
        xgT = sb("xgT", [P, 2, 2, Q * P], F32R)
        e_actT = sb("e_actT", [P, 2, Q * P])
        xg = sb("xg", [P, 2, Q, W])
        eg_act = sb("eg_act", [P, 2, Q, F])
        e_act = sb("e_act", [P, 2, Q, F])
        yg = sb("yg", [P, SLOT_TILES, D])
        home = sb("home", [P, SLOT_TILES], I32)
        away = sb("away", [P, SLOT_TILES])
        past = sb("past", [1, SLOT_TILES, E])

        bank = [ctx.enter_context(nc.psum_tensor(f"bank{i}", [P, 512], F32)) for i in range(4)]
        pair = ctx.enter_context(nc.psum_tensor("quad_banks", [P, 4, 512], F32))
        ps_xT, ps_qy, ps_vk, ps_log = bank
        ps_yT, ps_y = bank[0], bank[1]
        ps_gT, ps_aT, ps_yg = bank[3], bank[1], bank[2]
        setup_bank = bank[3]

        ld_x = [sem(f"ld_x{c}") for c in range(NQ)]
        ld_we = [sem(f"ld_we{n}") for n in range(E // EC)]
        ld_wd, ld_m = sem("ld_wd"), sem("ld_m")
        ld_b, ld_wo, ld_wa, ld_ws = sem("ld_b"), sem("ld_wo"), sem("ld_wa"), sem("ld_ws")
        we_hi, we_lo = sem("we_hi"), sem("we_lo")
        k_col, k_id, k_pool, k_ids = sem("k_col"), sem("k_id"), sem("k_pool"), sem("k_ids")
        z_done, zero_st = sem("z_done"), sem("zero_st")
        dch = sem("dch")
        ach = sem("ach")
        m_step = sem("m_step")
        var1, std1, rstd1 = sem("var1"), sem("std1"), sem("rstd1")
        center_rdy, wc_mm, wc_rdy, bo_add = sem("center_rdy"), sem("wc_mm"), sem("wc_rdy"), sem("bo_add")
        xT_mm, xT_sb = sem("xT_mm"), sem("xT_sb")
        qkv_mm, qkv_sb, sq_done, ss_done = sem("qkv_mm"), sem("qkv_sb"), sem("sq_done"), sem("ss_done")
        ssum, nrm, rn_rdy = sem("ssum"), sem("nrm"), sem("rn_rdy")
        v_rdy, q_rdy = sem("v_rdy"), sem("q_rdy")
        vk_mm, vkm_rdy, wb_mm, wb_rdy = sem("vk_mm"), sem("vkm_rdy"), sem("wb_mm"), sem("wb_rdy")
        qT_mm, qT_sb, y_mm, x1_rdy = sem("qT_mm"), sem("qT_sb"), sem("y_mm"), sem("x1_rdy")
        var2, std2, rstd2, h_rdy = sem("var2"), sem("std2"), sem("rstd2"), sem("h_rdy")
        su_mm, su_cp, su_lo, log_mm = sem("su_mm"), sem("su_cp"), sem("su_lo"), sem("log_mm")
        hT_hi_rdy, hT_rdy = sem("hT_hi_rdy"), sem("hT_rdy")
        top_rdy, score_rdy, hs_rdy, cnt_rdy, cnt_mm, pos_rdy, eid_rdy = (
            sem("top_rdy"), sem("score_rdy"), sem("hs_rdy"), sem("cnt_rdy"), sem("cnt_mm"), sem("pos_rdy"),
            sem("eid_rdy"))
        log_read = sem("log_read")
        hs_pool, scat = sem("hs_pool"), sem("scat")
        s_gu_mm, s_silu, s_act_rdy, s_hi, s_spl_rdy, s_dn_mm = (
            sem("s_gu_mm"), sem("s_silu"), sem("s_act_rdy"), sem("s_hi"), sem("s_spl_rdy"), sem("s_dn_mm"))
        yT_sb, yT_mm, y_free = sem("yT_sb"), sem("yT_mm"), sem("y_free")
        xg_ld = [sem("xg_ld0"), sem("xg_ld1")]
        gT_mm, gT_sb, e_gu_mm, e_silu, e_act_rdy = (
            sem("gT_mm"), sem("gT_sb"), sem("e_gu_mm"), sem("e_silu"), sem("e_act_rdy"))
        gT_hi = sem("gT_hi")
        aT_mm, aT_sb, e_dn_mm, yg_rdy = sem("aT_mm"), sem("aT_sb"), sem("e_dn_mm"), sem("yg_rdy")
        away_rdy, home_rdy, back = sem("away_rdy"), sem("home_rdy"), sem("back")
        ld_y = [sem(f"ld_y{c}") for c in range(NQ)]
        fin_pool = sem("fin_pool")
        fin, out_st = sem("fin"), sem("out_st")

        block = ctx.enter_context(nc.Block())

        def tiles(c):
            return range(Q * c, Q * c + Q)

        STEPS = NQ + 3
        SPLIT_STEPS = (2, 4, 6, 8)

        def live(c):
            return 0 <= c < NQ

        def attended(s):
            return [c for c in range(NQ) if min(c + 3, NQ + 1) == s]

        def turned(s):
            return [c for c in range(NQ) if min(c + 4, NQ + 2) == s]

        turns = [("x", 0), ("x", 1)]
        for s in range(1, STEPS):
            turns += [("h", c) for c in turned(s)] + [("x", s + 1)] * live(s + 1)
        turn_no = {turn: n + 1 for n, turn in enumerate(turns)}

        def slots(dram, g):
            return dram[bass.ds(g * (Q * P), Q * P), :].rearrange("(j p) d -> p j d", p=P)

        def gate_up_banks(par):
            return pair[:, 2 * par:2 * par + 2, :].rearrange("p a (b n) -> p (a b) n", b=2)

        def over_groups(step, eng, filler=lambda k: None):
            step(0, 1, (1, 0))
            step(1, 0, (2, 1, 0))
            step(1, 1, (3, 2, 1, 0))
            step(2, 0)
            step(2, 1)
            with eng.Fori(3, NG // 2) as i:
                step(i, 0)
                step(i, 1)
            step(NG // 2, 0, (3, 2, 1))
            filler(0)
            step(NG // 2, 1, (3, 2))
            filler(1)
            step(NG // 2 + 1, 0, (3,))

        @block.sync
        def _(sp):
            for c in range(NQ):
                sp.dma_start(xres[:, Q * c:Q * c + Q, :], x_rows[:, Q * c:Q * c + Q, :]).then_inc(ld_x[c], 16)
                if c == 0:
                    for n, b in enumerate((bq, bk, bv)):
                        sp.dma_start(b_qkv[:, D * n:D * n + D], b.partition_broadcast(P)).then_inc(ld_b, 16)
                if c == 1:
                    sp.dma_start(b_o[:], bo.partition_broadcast(P)).then_inc(ld_wo, 16)
                    sp.dma_start(w_o[:], Wo).then_inc(ld_wo, 16)
            sp.dma_start(sg_in[:], shared_gate.rearrange("(k f) h -> f k h", f=P)).then_inc(ld_ws, 16)
            sp.dma_start(su_in[:], shared_up.rearrange("(k f) h -> f k h", f=P)).then_inc(ld_ws, 16)
            sp.dma_start(sd_in[:], shared_down).then_inc(ld_ws, 16)
            sp.dma_start(rw_in[:], router_w).then_inc(ld_ws, 16)
            sp.wait_ge(z_done, 1)
            rows = x_slots.rearrange("(p r) d -> p (r d)", p=P)
            zeros = w_raw[:, 1].rearrange("p e n -> p (e n)")
            for i in range(ZERO_LOADS):
                sp.dma_start(rows[:, i * ZW:(i + 1) * ZW], zeros[:, 0:ZW]).then_inc(zero_st, 16)
            for n in range(E // EC):
                if n == 1:
                    sp.wait_ge(zero_st, 16 * ZERO_LOADS)
                if n >= 2:
                    sp.wait_ge(we_lo, n - 1)
                e = slice(n * EC, n * EC + EC)
                sp.dma_start(w_raw[:, n % 2], gate_up[e].rearrange("e h f -> h e f")).then_inc(ld_we[n], 16)
            sp.dma_start(w_dn[:], down.rearrange("e f h -> f e h")).then_inc(ld_wd, 16)

            def load_group(g, par):
                sp.dma_start(xg[:, par], slots(x_slots, g)).then_inc(xg_ld[par], 16)

            def experts(i, par, stages=(3, 2, 1, 0)):
                g = i * 2 + par
                if 0 in stages:
                    if not (isinstance(i, int) and g < 2):
                        sp.wait_ge(gT_mm, g - 1)
                        sp.wait_ge(home_rdy, g - 1)
                    load_group(g, par)

            sp.wait_ge(scat, 16 * NT)
            experts(0, 0, (0,))
            over_groups(experts, sp)
            sp.wait_ge(back, 16 * SLOT_TILES)
            y_home = y_rows[1:1 + T, :].rearrange("(j p) d -> p j d", p=P)
            for c in [c for two in zip(range(POOL_FINAL), range(POOL_FINAL, NQ)) for c in two]:
                sp.dma_start(h_rows[:, Q * c:Q * c + Q, 0:D], y_home[:, Q * c:Q * c + Q, :]).then_inc(ld_y[c], 16)
            for c in range(POOL_FINAL):
                sp.wait_ge(fin_pool, c + 1)
                sp.dma_start(out_rows[:, Q * c:Q * c + Q, :], xres[:, Q * c:Q * c + Q, :]).then_inc(out_st, 16)
            sp.wait_ge(out_st, 16 * NQ)

        @block.gpsimd
        def _(pool):
            g = nc.gpsimd
            g.memset(eps_col[:], EPS)
            g.memset(zero_col[:], 0.0).then_inc(k_col, 1)
            g.memset(ident[:], 0.0)
            g.memset(before[:], 1.0)
            g.memset(ones[:], 1.0)
            g.memset(head_mask[:], 1.0)
            for mask in run_mask:
                g.memset(mask[:], 1.0)
            g.memset(w_raw[:, 1], 0.0).then_inc(z_done, 1)
            pool.wait_ge(z_done, 1)
            g.affine_select(out=ident[:], in_=ident[:], compare_op=ALU.not_equal, fill=1.0, base=0,
                            pattern=[[-1, P]], channel_multiplier=1).then_inc(k_id, 1)
            g.affine_select(out=before[:], in_=before[:], compare_op=ALU.is_gt, fill=0.0, base=0,
                            pattern=[[1, P]], channel_multiplier=-1)
            g.affine_select(out=head_mask[:], in_=head_mask[:], compare_op=ALU.is_ge, fill=0.0, base=0,
                            pattern=[[-HD, HEADS], [0, HD]], channel_multiplier=1).then_inc(k_pool, 1)
            for mask, n in zip(run_mask, sizes):
                g.affine_select(out=mask[:], in_=mask[:], compare_op=ALU.not_equal, fill=0.0, base=0,
                                pattern=[[0, E], [1, n]], channel_multiplier=0)
            g.iota(h_rows[:, :, D], pattern=[[P, NT]], base=1, channel_multiplier=1,
                   allow_small_or_imprecise_dtypes=True).then_inc(k_ids, 1)
            g.iota(free_row[:], pattern=[[P, SLOT_TILES]], base=1 + T, channel_multiplier=1,
                   allow_small_or_imprecise_dtypes=True).then_inc(k_ids, 1)
            g.iota(rank_key[:], pattern=[[0, NT], [-1, E]], base=E, channel_multiplier=0,
                   allow_small_or_imprecise_dtypes=True)
            g.iota(tile_no[:], pattern=[[1, SLOT_TILES], [0, E]], base=0, channel_multiplier=0,
                   allow_small_or_imprecise_dtypes=True)
            pool.wait_ge(k_pool, 1)
            g.affine_select(out=head_mask[:], in_=head_mask[:], compare_op=ALU.is_ge, fill=0.0, base=HD - 1,
                            pattern=[[HD, HEADS], [0, HD]], channel_multiplier=-1).then_inc(k_pool, 1)

            def scale_heads(c, col, r_col, done):
                pool.wait_ge(rn_rdy, c + 1)
                v = qkv[:, c % QRING, :, col:col + D].rearrange("p j (n d) -> p j n d", d=HD)
                r = rn[:, c % 2, :, r_col:r_col + HEADS].unsqueeze(3).broadcast_to([P, Q, HEADS, HD])
                g.tensor_tensor(v, v, r, ALU.mult).then_inc(done, 1)

            def add_bo(c):
                if c == 0:
                    pool.wait_ge(ld_wo, 16 * 2)
                pool.wait_ge(var1, c + 1)
                pool.wait_ge(xT_mm, turn_no["x", c])
                r = xres[:, Q * c:Q * c + Q, :]
                g.tensor_tensor(r, r, b_o[:].unsqueeze(1).broadcast_to([P, Q, D]), ALU.add).then_inc(bo_add, 1)

            def hT_lo(c):
                pool.wait_ge(hT_hi_rdy, c + 1)
                g.tensor_tensor(hT[:, 1, 512 * c:512 * c + 512], hT_raw[:, c % 2],
                                hT[:, 0, 512 * c:512 * c + 512].bitcast(F32), ALU.subtract).then_inc(hT_rdy, 1)

            def split_lo(n):
                e = slice(n * EC, n * EC + EC)
                pool.wait_ge(we_hi, n + 1)
                g.tensor_tensor(w_gu[:, 1, e, :], w_raw[:, n % 2], w_gu[:, 0, e, :].bitcast(F32), ALU.subtract
                                ).then_inc(we_lo, 1)

            def scale_h(c):
                t = slice(Q * c, Q * c + Q)
                pool.wait_ge(score_rdy, 1)
                pool.wait_ge(xT_mm, turn_no["h", c])
                g.tensor_tensor(h_rows[:, t, 0:D], h_rows[:, t, 0:D], score[:, t].unsqueeze(2).broadcast_to([P, Q, D]),
                                ALU.mult).then_inc(hs_pool, 1)

            for s in range(STEPS):
                if live(s - 1):
                    scale_heads(s - 1, 2 * D, HEADS, v_rdy)
                    scale_heads(s - 1, 0, 0, q_rdy)
                for c in turned(s):
                    hT_lo(c)
                if live(s - 1):
                    add_bo(s - 1)
                if s in SPLIT_STEPS:
                    split_lo(SPLIT_STEPS.index(s))

            for c in range(POOL_QUADS):
                scale_h(c)
            pool.wait_ge(zero_st, 16 * ZERO_LOADS)
            pool.wait_ge(k_ids, 2)
            for t in range(NT):
                pool.wait_ge(pos_rdy, 1 if t < Q * EARLY else 2)
                if t < Q * POOL_QUADS:
                    pool.wait_ge(hs_pool, t // Q + 1)
                else:
                    pool.wait_ge(hs_rdy, t - Q * POOL_QUADS + 1)
                g.indirect_dma_start(out=x_slots, out_offset=bass.IndirectOffsetOnAxis(ap=pos[:, t:t + 1], axis=0),
                                     in_=h_rows[:, t, :], in_offset=None).then_inc(scat, 16)
            for g_no in range(NG):
                pool.wait_ge(home_rdy, g_no + 1)
                pool.wait_ge(yg_rdy, g_no + 1)
                for n in range(Q * g_no, Q * g_no + Q):
                    g.indirect_dma_start(out=y_rows, out_offset=bass.IndirectOffsetOnAxis(ap=home[:, n:n + 1], axis=0),
                                         in_=yg[:, n, :], in_offset=None).then_inc(back, 16)
            for c in range(POOL_FINAL):
                pool.wait_ge(ld_y[c], 16)
                pool.wait_ge(y_free, c + 2)
                r = xres[:, Q * c:Q * c + Q, :]
                g.tensor_tensor(r, r, h_rows[:, Q * c:Q * c + Q, 0:D], ALU.add).then_inc(fin_pool, 1)

        @block.scalar
        def _(act):
            a = nc.scalar
            act.dma_start(m_col[:], m.unsqueeze(1).broadcast_to([HEADS, HD])).then_inc(ld_m, 16)
            for dst, src in ((w_qkv[:, 0:D], Wq), (w_qkv[:, D:2 * D], Wk), (w_qkv[:, 2 * D:QKV], Wv)):
                act.dma_start(dst, src).then_inc(ld_wa, 16)
            act.wait_ge(xT_mm, turn_no["x", 0])
            a.copy(xT[:, 0], ps_xT[:]).then_inc(xT_sb, 1)
            act.wait_ge(ld_m, 16)
            act.wait_ge(k_col, 1)
            a.activation(m_tmp[:, 0:1], m_col[:], ACT.Exp, bias=zero_col[:], scale=-1.0).then_inc(ach, 1)
            act.wait_ge(m_step, 1)
            a.activation(m_tmp[:, 3:4], m_tmp[:, 2:3], ACT.Exp, bias=zero_col[:],
                         scale=-float(np.log(S))).then_inc(ach, 1)

            def std(dst, mv, var, done, c):
                t = slice(Q * c, Q * c + Q)
                act.wait_ge(var, c + 1)
                a.activation(dst[:, t], mv[:, t, 1], ACT.Sqrt, bias=eps_col[:], scale=1.0).then_inc(done, 1)

            def norm_h(c):
                act.wait_ge(rstd2, c + 1)
                for t in tiles(c):
                    last = a.activation(h_rows[:, t, 0:D], xres[:, t, :], ACT.Identity, bias=nm2[:, t:t + 1],
                                        scale=rs2[:, t:t + 1])
                last.then_inc(h_rdy, 1)

            def xT_copy(c):
                act.wait_ge(xT_mm, turn_no["x", c])
                if c >= 2:
                    act.wait_ge(qkv_mm, 2 * (c - 1))
                a.copy(xT[:, c % 2], ps_xT[:]).then_inc(xT_sb, 1)

            def hT_hi(c):
                act.wait_ge(xT_mm, turn_no["h", c])
                if c >= 2:
                    act.wait_ge(hT_rdy, c - 1)
                a.copy(hT_raw[:, c % 2], ps_xT[:]).then_inc(xT_sb, 1)
                act.wait_ge(xT_sb, turn_no["h", c])
                a.copy(hT[:, 0, 512 * c:512 * c + 512], hT_raw[:, c % 2]).then_inc(hT_hi_rdy, 1)

            def square(c):
                act.wait_ge(qkv_sb, 2 * (c + 1))
                if c >= 1:
                    act.wait_ge(ss_done, c)
                a.activation(sq[:], qkv[:, c % QRING, :, 0:2 * D], ACT.Square).then_inc(sq_done, 1)

            def head_norms(c):
                act.wait_ge(ssum, c + 1)
                if c >= 2:
                    act.wait_ge(q_rdy, c - 1)
                a.activation(rn[:, c % 2], ss[:, c % 2], ACT.Sqrt).then_inc(nrm, 1)

            def qT_copy(c):
                act.wait_ge(qT_mm, c + 1)
                if c >= RING:
                    act.wait_ge(y_mm, c - RING + 1)
                a.copy(qT[:, c % RING], ps_qy[:]).then_inc(qT_sb, 1)

            def wb_copy(b):
                act.wait_ge(wb_mm, b + 1)
                if b >= 2:
                    act.wait_ge(y_mm, QB * (b - 1))
                a.copy(wb[:, b % 2], ps_vk[:, D:2 * D]).then_inc(wb_rdy, 1)

            def split_hi(n):
                act.wait_ge(ld_we[n], 16)
                a.copy(w_gu[:, 0, n * EC:n * EC + EC, :], w_raw[:, n % 2]).then_inc(we_hi, 1)

            def weights_hi(n):
                act.wait_ge(su_mm, n + 1)
                dst = (sgT, suT, sdT, rwT)[n][:, 0]
                a.copy(dst, setup_bank[:, 0:dst.shape[1]]).then_inc(su_cp, 1)

            def take_scores(i):
                act.wait_ge(top_rdy, i + 1)
                a.activation(score[:, PARTS[i]], top[:, PARTS[i]], ACT.Sigmoid).then_inc(score_rdy, 1)

            def silu_shared(c, k):
                n = c * KC + k
                act.wait_ge(s_gu_mm, n + 1)
                a.activation(sg_act[:, k % 2], pair[:, 2 * (k % 2)], ACT.Silu).then_inc(s_silu, 1)

            def hi_shared(c, k):
                act.wait_ge(s_act_rdy, c * KC + k + 1)
                if not (isinstance(c, int) and c == 0 and k < 2):
                    act.wait_ge(s_dn_mm, c * KC + k - 1)
                a.copy(s_spl[:, k % 2, 0], s_act[:, k % 2]).then_inc(s_hi, 1)

            act.wait_ge(wc_mm, 1)
            a.copy(w_c[:], pair[:, 0, 0:QKV]).then_inc(wc_rdy, 1)
            std(rs1, mv1, var1, std1, 0)
            xT_copy(1)
            for s in range(STEPS):
                if live(s + 1):
                    std(rs1, mv1, var1, std1, s + 1)
                if s in SPLIT_STEPS:
                    split_hi(SPLIT_STEPS.index(s))
                for c in turned(s):
                    hT_hi(c)
                if 1 <= s < 5:
                    weights_hi(s - 1)
                if live(s):
                    square(s)
                if live(s - 1):
                    qT_copy(s - 1)
                if attended(s):
                    std(rs2, mv2, var2, std2, attended(s)[0])
                if s >= 1 and live(s + 1):
                    xT_copy(s + 1)
                if live(s):
                    head_norms(s)
                if attended(s):
                    norm_h(attended(s)[0])
                if s == NQ + 1:
                    std(rs2, mv2, var2, std2, NQ - 1)
                    norm_h(NQ - 1)
                if live(s - 1) and (s - 1) % 2:
                    wb_copy((s - 1) // 2)

            silu_shared(0, 0)
            silu_shared(0, 1)
            hi_shared(0, 0)
            hi_shared(0, 1)
            silu_shared(0, 2)
            take_scores(0)
            take_scores(1)
            act.wait_ge(score_rdy, 2)
            act.wait_ge(xT_mm, 2 * NQ)
            for t in range(Q * POOL_QUADS, NT):
                row = h_rows[:, t, 0:D]
                a.activation(row, row, ACT.Copy, scale=score[:, t:t + 1]).then_inc(hs_rdy, 1)
            hi_shared(0, 2)
            silu_shared(0, 3)

            def yT_copy(c):
                act.wait_ge(s_dn_mm, (c + 1) * KC)
                a.copy(yT[:], ps_yT[:]).then_inc(yT_sb, 1)

            def shared(lo, hi):
                if lo > 0:
                    hi_shared(lo, 0)
                    for k in range(2, KC):
                        silu_shared(lo, k)
                        hi_shared(lo, k - 1)
                with act.Fori(lo + 1, hi) as c:
                    silu_shared(c, 0)
                    hi_shared(c - 1, KC - 1)
                    silu_shared(c, 1)
                    hi_shared(c, 0)
                    yT_copy(c - 1)
                    for k in range(2, KC):
                        silu_shared(c, k)
                        hi_shared(c, k - 1)
                hi_shared(hi - 1, KC - 1)
                if hi < NQ:
                    experts(0, 0, (0,))
                yT_copy(hi - 1)

            def experts(i, par, stages=(3, 2, 1, 0)):
                g = i * 2 + par
                if 0 in stages:
                    act.wait_ge(gT_mm, g + 1)
                    a.copy(xgT[:, par, 0], ps_gT[:]).then_inc(gT_hi, 1)
                if 1 in stages:
                    act.wait_ge(e_gu_mm, g)
                    a.activation(eg_act[:, (par - 1) % 2], gate_up_banks((par - 1) % 2)[:, :, 0:F],
                                 ACT.Silu).then_inc(e_silu, 1)
                if 3 in stages:
                    act.wait_ge(e_dn_mm, g - 2)
                    a.copy(yg[:, bass.ds((g - 3) * Q, Q), :], ps_yg[:].rearrange("p (j d) -> p j d", d=D)
                           ).then_inc(yg_rdy, 1)

            shared(0, C1)
            over_groups(experts, act, lambda k: silu_shared(C1, k))
            shared(C1, NQ)
            for c in range(POOL_FINAL, NQ):
                act.wait_ge(fin, c - POOL_FINAL + 1)
                act.dma_start(out_rows[:, Q * c:Q * c + Q, :], xres[:, Q * c:Q * c + Q, :]).then_inc(out_st, 16)

        @block.vector
        def _(dve):
            v = nc.vector
            links = [0]

            def link(ins):
                links[0] += 1
                ins.then_inc(dch, 1)
                dve.wait_ge(dch, links[0])

            def stats(c, st, mv, done):
                for t in tiles(c):
                    last = v.bn_stats(st[:, t, :], xres[:, t, :])
                link(last)
                for t in tiles(c):
                    last = v.bn_aggr(mv[:, t, :], st[:, t, :])
                last.then_inc(done, 1)

            def x_stats(c):
                dve.wait_ge(ld_x[c], 16)
                stats(c, st1, mv1, var1)

            def x_scales(c):
                t = slice(Q * c, Q * c + Q)
                dve.wait_ge(std1, c + 1)
                v.reciprocal(rs1[:, t], rs1[:, t]).then_inc(rstd1, 1)

            def h_scales(c):
                t = slice(Q * c, Q * c + Q)
                dve.wait_ge(std2, c + 1)
                link(v.reciprocal(rs2[:, t], rs2[:, t]))
                v.scalar_tensor_tensor(out=nm2[:, t], in0=mv2[:, t, 0], scalar=-1.0, in1=rs2[:, t], op0=ALU.mult,
                                       op1=ALU.mult).then_inc(rstd2, 1)

            def take_qkv(c):
                if c == 0:
                    dve.wait_ge(ld_b, 16 * 3)
                dve.wait_ge(rstd1, c + 1)
                if c >= QRING:
                    dve.wait_ge(qT_mm, c - QRING + 1)
                    dve.wait_ge(vk_mm, c - QRING + 1)
                for j, t in enumerate(tiles(c)):
                    if j % 2 == 0:
                        dve.wait_ge(qkv_mm, 2 * c + j // 2 + 1)
                    last = v.scalar_tensor_tensor(out=qkv[:, c % QRING, j, :], in0=pair[:, j, 0:QKV],
                                                  scalar=rs1[:, t:t + 1], in1=b_qkv[:], op0=ALU.mult, op1=ALU.add)
                    if j % 2:
                        last.then_inc(qkv_sb, 1)

            def head_sums(c):
                dve.wait_ge(sq_done, c + 1)
                if c >= 2:
                    dve.wait_ge(nrm, c - 1)
                v.tensor_reduce(ss[:, c % 2], sq[:].rearrange("p j (n d) -> p j n d", d=HD), AX.X, ALU.add
                                ).then_inc(ss_done, 1)
                dve.wait_ge(ss_done, c + 1)
                v.tensor_scalar(ss[:, c % 2], ss[:, c % 2], 1e-24, None, ALU.max).then_inc(ssum, 1)

            def inv_norms(c):
                dve.wait_ge(nrm, c + 1)
                v.reciprocal(rn[:, c % 2], rn[:, c % 2]).then_inc(rn_rdy, 1)

            def mask_vk(b):
                dve.wait_ge(vk_mm, QB * (b + 1))
                if b >= 2:
                    dve.wait_ge(wb_mm, b - 1)
                v.tensor_tensor(vkm[:, b % 2], ps_vk[:, 0:D], head_mask[:], ALU.mult).then_inc(vkm_rdy, 1)

            def add_attn(c):
                dve.wait_ge(y_mm, c + 1)
                dve.wait_ge(bo_add, c + 1)
                r = xres[:, Q * c:Q * c + Q, :]
                v.tensor_tensor(r, ps_qy[:].rearrange("p (j d) -> p j d", d=D), r, ALU.add).then_inc(x1_rdy, 1)
                dve.wait_ge(x1_rdy, c + 1)
                stats(c, st2, mv2, var2)

            def weights_lo(n):
                dve.wait_ge(su_cp, n + 1)
                w = (sgT, suT, sdT, rwT)[n]
                v.tensor_tensor(w[:, 1], setup_bank[:, 0:w.shape[2]], w[:, 0].bitcast(F32), ALU.subtract
                                ).then_inc(su_lo, 1)

            def act_shared(c, k):
                dve.wait_ge(s_silu, c * KC + k + 1)
                if not (isinstance(c, int) and c == 0 and k < 2):
                    dve.wait_ge(s_spl_rdy, c * KC + k - 1)
                v.tensor_tensor(s_act[:, k % 2], pair[:, 2 * (k % 2) + 1], sg_act[:, k % 2], ALU.mult
                                ).then_inc(s_act_rdy, 1)

            def lo_shared(c, k):
                dve.wait_ge(s_hi, c * KC + k + 1)
                v.tensor_tensor(s_spl[:, k % 2, 1], s_act[:, k % 2], s_spl[:, k % 2, 0].bitcast(F32), ALU.subtract
                                ).then_inc(s_spl_rdy, 1)

            dve.wait_ge(k_id, 1)
            v.tensor_scalar(center[:], ident[:], -1.0 / D, None, ALU.add).then_inc(center_rdy, 1)
            x_stats(0)
            dve.wait_ge(ach, 1)
            link(v.tensor_scalar(m_tmp[:, 1:2], m_tmp[:, 0:1], 1.0, None, ALU.add))
            v.reciprocal(m_tmp[:, 2:3], m_tmp[:, 1:2]).then_inc(m_step, 1)
            x_stats(1)
            x_scales(0)
            for s in range(STEPS):
                if live(s):
                    take_qkv(s)
                if s == 0:
                    dve.wait_ge(ach, 2)
                    dve.wait_ge(k_pool, 2)
                    link(v.tensor_scalar(head_mask[:], head_mask[:], m_tmp[:, 3:4], None, ALU.mult))
                if attended(s):
                    add_attn(attended(s)[0])
                if live(s - 1) and (s - 1) % 2:
                    mask_vk((s - 1) // 2)
                if 1 <= s < 5:
                    weights_lo(s - 1)
                if live(s):
                    head_sums(s)
                if live(s + 1):
                    x_scales(s + 1)
                if attended(s):
                    h_scales(attended(s)[0])
                if s == NQ + 1:
                    add_attn(NQ - 1)
                    h_scales(NQ - 1)
                if live(s + 2):
                    x_stats(s + 2)
                if live(s):
                    inv_norms(s)
            v.engine_nop().then_inc(y_free, 1)

            logits = ps_log[:].rearrange("p (t e) -> p t e", e=E)

            def choose(i):
                t, n = PARTS[i], sizes[i]
                dve.wait_ge(log_mm, t.stop // Q)
                v.tensor_reduce(top[:, t], logits[:, t, :], AX.X, ALU.max).then_inc(top_rdy, 1)
                dve.wait_ge(top_rdy, i + 1)
                v.tensor_tensor(key[i], logits[:, t, :], top[:, t].unsqueeze(2).broadcast_to([P, n, E]), ALU.is_equal
                                ).then_inc(log_read, 1)
                dve.wait_ge(log_read, i + 1)
                link(v.tensor_tensor(key[i], key[i], rank_key[:, t, :], ALU.mult))
                link(v.tensor_reduce(ktop[i][:], key[i], AX.X, ALU.max))
                link(v.tensor_tensor(hot[i][:].rearrange("p e t -> p t e"), key[i],
                                     ktop[i][:].unsqueeze(2).broadcast_to([P, n, E]), ALU.is_equal))
                link(v.tensor_reduce(cnt_part[:, i], hot[i][:], AX.X, ALU.add))

            def count_ahead(i):
                link(v.tensor_tensor_scan(run[i][:].rearrange("p e t -> p (e t)"),
                                          run_mask[i][:].rearrange("p e t -> p (e t)"),
                                          hot[i][:].rearrange("p e t -> p (e t)"), 0.0, ALU.mult, ALU.add))
                link(v.tensor_tensor(run[i][:], run[i][:], hot[i][:], ALU.mult))
                link(v.tensor_reduce(ahead[:, PARTS[i]], run[i][:].rearrange("p e t -> p t e"), AX.X, ALU.add))

            def place(i):
                link(v.tensor_tensor(run[i][:], hot[i][:], base[:, i].unsqueeze(2).broadcast_to([P, E, sizes[i]]),
                                     ALU.mult))
                link(v.tensor_reduce(first[:, PARTS[i]], run[i][:].rearrange("p e t -> p t e"), AX.X, ALU.add))
                v.tensor_tensor(pos[:, PARTS[i]], first[:, PARTS[i]], ahead[:, PARTS[i]], ALU.add).then_inc(pos_rdy, 1)

            dve.wait_ge(k_pool, 2)
            choose(0)
            act_shared(0, 0)
            act_shared(0, 1)
            lo_shared(0, 0)
            count_ahead(0)
            lo_shared(0, 1)
            choose(1)
            v.tensor_tensor(cnt[:], cnt_part[:, 0], cnt_part[:, 1], ALU.add).then_inc(cnt_rdy, 1)
            act_shared(0, 2)
            count_ahead(1)
            dve.wait_ge(cnt_mm, 1)
            link(v.tensor_scalar(tot_i[:], ps_vk[:, 32:32 + E], float(P - 1), None, ALU.add))
            link(v.tensor_scalar(til_i[:], tot_i[:], P.bit_length() - 1, None, ALU.logical_shift_right))
            link(v.tensor_copy(til[:], til_i[:]))
            link(v.tensor_tensor_scan(til_end[:], ones[:, 0:E], til[:], 0.0, ALU.mult, ALU.add))
            link(v.tensor_tensor(base[:, 0], til_end[:], til[:], ALU.subtract))
            link(v.tensor_scalar(base[:, 0], base[:, 0], float(P), -1.0, ALU.mult, ALU.add))
            link(v.tensor_tensor(base[:, 0], ps_vk[:, 0:E], base[:, 0], ALU.add))
            link(v.tensor_tensor(base[:, 1], cnt_part[:, 0], base[:, 0], ALU.add))
            place(0)
            place(1)
            lo_shared(0, 2)
            act_shared(0, 3)
            link(v.tensor_tensor(past[:], til_end[0:1, :].unsqueeze(1).broadcast_to([1, SLOT_TILES, E]), tile_no[:],
                                 ALU.is_le))
            link(v.tensor_reduce(eid_f[:], past[:], AX.X, ALU.add))
            by_group = eid_f[:].rearrange("o (g j) -> o g j", j=Q)
            v.tensor_scalar(eid[:, 3:NG + 3, 0], by_group, float(E - 1), float(D), ALU.min, ALU.mult
                            ).then_inc(eid_rdy, 1)
            v.tensor_scalar(eid[:, 1:NG + 1, 1], by_group, float(E - 1), float(D), ALU.min, ALU.mult
                            ).then_inc(eid_rdy, 1)

            def add_experts(c):
                dve.wait_ge(ld_y[c], 16)
                dve.wait_ge(y_free, c + 2)
                r = xres[:, Q * c:Q * c + Q, :]
                v.tensor_tensor(r, r, h_rows[:, Q * c:Q * c + Q, 0:D], ALU.add).then_inc(fin, 1)

            def add_shared(c):
                dve.wait_ge(yT_mm, c + 1)
                r = xres[:, bass.ds(c * Q, Q), :]
                v.tensor_tensor(r, ps_y[:].rearrange("p (j d) -> p j d", d=D), r, ALU.add).then_inc(y_free, 1)

            def shared(lo, hi):
                if lo > 0:
                    lo_shared(lo, 0)
                    for k in range(2, KC):
                        act_shared(lo, k)
                        lo_shared(lo, k - 1)
                with dve.Fori(lo + 1, hi) as c:
                    act_shared(c, 0)
                    lo_shared(c - 1, KC - 1)
                    act_shared(c, 1)
                    lo_shared(c, 0)
                    act_shared(c, 2)
                    lo_shared(c, 1)
                    add_shared(c - 1)
                    act_shared(c, 3)
                    lo_shared(c, 2)
                lo_shared(hi - 1, KC - 1)
                if hi < NQ:
                    dve.wait_ge(k_ids, 2)
                    experts(0, 0, (0,))
                else:
                    for c in range(POOL_FINAL, NQ - 1):
                        add_experts(c)
                add_shared(hi - 1)

            def experts(i, par, stages=(3, 2, 1, 0)):
                g = i * 2 + par
                if 0 in stages:
                    dve.wait_ge(xg_ld[par], (i + 1) * 16)
                    here = bass.ds(g * Q, Q)
                    v.scalar_tensor_tensor(out=away[:, here], in0=xg[:, par, :, D], scalar=0.0, in1=free_row[:, here],
                                           op0=ALU.is_equal, op1=ALU.mult).then_inc(away_rdy, 1)
                    dve.wait_ge(away_rdy, g + 1)
                    v.tensor_tensor(home[:, here], xg[:, par, :, D], away[:, here], ALU.add).then_inc(home_rdy, 1)
                    dve.wait_ge(gT_hi, g + 1)
                    v.tensor_tensor(xgT[:, par, 1], ps_gT[:], xgT[:, par, 0].bitcast(F32), ALU.subtract
                                    ).then_inc(gT_sb, 1)
                if 1 in stages:
                    dve.wait_ge(e_silu, g)
                    v.tensor_tensor(e_act[:, (par - 1) % 2], gate_up_banks((par - 1) % 2)[:, :, F:F2],
                                    eg_act[:, (par - 1) % 2], ALU.mult).then_inc(e_act_rdy, 1)
                if 2 in stages:
                    dve.wait_ge(aT_mm, g - 1)
                    v.tensor_copy(e_actT[:, par], ps_aT[:]).then_inc(aT_sb, 1)

            shared(0, C1)
            over_groups(experts, dve, lambda k: act_shared(C1, k))
            shared(C1, NQ)
            add_experts(NQ - 1)

        @block.tensor
        def _(pe):
            te = nc.tensor
            pe.wait_ge(k_id, 1)

            def center_weights():
                pe.wait_ge(center_rdy, 1)
                pe.wait_ge(ld_wa, 16 * 3)
                te.matmul(pair[:, 0, 0:QKV], center[:], w_qkv[:], start=True, stop=True).then_inc(wc_mm, 1)

            def turn(src, kind, c):
                n = turn_no[kind, c]
                if kind == "x":
                    pe.wait_ge(ld_x[c], 16)
                else:
                    pe.wait_ge(h_rdy, c + 1)
                if n > 1:
                    pe.wait_ge(xT_sb, n - 1)
                for j, t in enumerate(tiles(c)):
                    last = te.transpose(ps_xT[:, P * j:P * j + P], src[:, t, 0:D], ident[:])
                last.then_inc(xT_mm, 1)

            def project(c):
                if c == 0:
                    pe.wait_ge(wc_rdy, 1)
                pe.wait_ge(xT_sb, turn_no["x", c])
                for j in range(Q):
                    if j % 2 == 0 and c >= 1:
                        pe.wait_ge(qkv_sb, 2 * (c - 1) + j // 2 + 1)
                    last = te.matmul(pair[:, j, 0:QKV], xT[:, c % 2, P * j:P * j + P], w_c[:], start=True, stop=True)
                    if j % 2:
                        last.then_inc(qkv_mm, 1)

            def v_by_k(c):
                b, h = divmod(c, QB)
                if h == 0 and b >= 1:
                    pe.wait_ge(wb_rdy, b)
                pe.wait_ge(v_rdy, c + 1)
                for j in range(Q):
                    last = te.matmul(ps_vk[:, 0:D], qkv[:, c % QRING, j, 2 * D:QKV], qkv[:, c % QRING, j, D:2 * D],
                                     start=(h == 0 and j == 0), stop=(h == QB - 1 and j == Q - 1))
                last.then_inc(vk_mm, 1)

            def fold_wo(b):
                if b == 0:
                    pe.wait_ge(ld_wo, 16 * 2)
                pe.wait_ge(vkm_rdy, b + 1)
                te.matmul(ps_vk[:, D:2 * D], vkm[:, b % 2], w_o[:], start=True, stop=True).then_inc(wb_mm, 1)

            def turn_q(c):
                pe.wait_ge(q_rdy, c + 1)
                if c >= 2:
                    pe.wait_ge(x1_rdy, c - 1)
                if c >= 1:
                    pe.wait_ge(qT_sb, c)
                for j in range(Q):
                    last = te.transpose(ps_qy[:, P * j:P * j + P], qkv[:, c % QRING, j, 0:D], ident[:])
                last.then_inc(qT_mm, 1)

            def attend(c):
                pe.wait_ge(qT_sb, min(c + 2, NQ))
                pe.wait_ge(wb_rdy, c // QB + 1)
                if c >= 1:
                    pe.wait_ge(x1_rdy, c)
                for j in range(Q):
                    last = te.matmul(ps_qy[:, P * j:P * j + P], qT[:, c % RING, P * j:P * j + P], wb[:, c // QB % 2],
                                     start=True, stop=True)
                last.then_inc(y_mm, 1)

            def split_product(out, lhs, rhs):
                te.matmul(out, lhs[:, 0], rhs[:, 0], start=True, stop=False)
                te.matmul(out, lhs[:, 0], rhs[:, 1], start=False, stop=False)
                return te.matmul(out, lhs[:, 1], rhs[:, 0], start=False, stop=True)

            def route(c):
                pe.wait_ge(hT_rdy, c + 1)
                if c == EARLY:
                    pe.wait_ge(log_read, 1)
                for t in tiles(c):
                    last = split_product(ps_log[:, E * t:E * t + E], hT[:, :, P * t:P * t + P], rwT)
                last.then_inc(log_mm, 1)

            def turn_weights(n):
                if n == 0:
                    pe.wait_ge(ld_ws, 16 * 4)
                else:
                    pe.wait_ge(su_lo, n)
                if n == 3:
                    last = te.transpose(setup_bank[:, 0:E], rw_in[:], ident[0:E, 0:E])
                else:
                    for k in range(KC):
                        src = (sg_in[:, k, :], su_in[:, k, :], sd_in[:, P * k:P * k + P])[n]
                        last = te.transpose(setup_bank[:, P * k:P * k + P], src, ident[:])
                last.then_inc(su_mm, 1)

            def gate_up_shared(c, k):
                n = c * KC + k
                if not (isinstance(c, int) and n < 2):
                    pe.wait_ge(s_act_rdy, n - 1)
                h = hT[:, :, bass.ds(c * 512, 512)]
                split_product(pair[:, 2 * (k % 2)], sgT[:, :, P * k:P * k + P], h)
                split_product(pair[:, 2 * (k % 2) + 1], suT[:, :, P * k:P * k + P], h).then_inc(s_gu_mm, 1)

            def down_shared(c, k):
                pe.wait_ge(s_spl_rdy, c * KC + k + 1)
                if k == 0 and not (isinstance(c, int) and c == 0):
                    pe.wait_ge(yT_sb, c)
                w, h = sdT[:, :, D * k:D * k + D], s_spl[:, k % 2]
                te.matmul(ps_yT[:], w[:, 0], h[:, 0], start=(k == 0), stop=False)
                te.matmul(ps_yT[:], w[:, 1], h[:, 0], start=False, stop=False)
                te.matmul(ps_yT[:], w[:, 0], h[:, 1], start=False, stop=(k == KC - 1)).then_inc(s_dn_mm, 1)

            turn(xres, "x", 0)
            turn(xres, "x", 1)
            center_weights()
            for s in range(STEPS):
                if live(s):
                    project(s)
                for c in attended(s):
                    attend(c)
                    if c == NQ - 2:
                        turn(h_rows, "h", c - 1)
                if s == NQ + 1:
                    pe.wait_ge(qkv_sb, 2 * NQ)
                    gate_up_shared(0, 0)
                else:
                    for c in turned(s):
                        turn(h_rows, "h", c)
                    if s == NQ + 2:
                        gate_up_shared(0, 1)
                if live(s - 1):
                    v_by_k(s - 1)
                    turn_q(s - 1)
                if s >= 1 and live(s + 1):
                    turn(xres, "x", s + 1)
                if s < 4:
                    turn_weights(s)
                if s == NQ:
                    fold_wo(NQ // QB - 1)
                for c in turned(s):
                    if c == 0:
                        pe.wait_ge(su_lo, 4)
                    route(c)
                if live(s) and s >= 1 and (s - 1) % 2:
                    fold_wo((s - 1) // 2)

            gate_up_shared(0, 2)
            down_shared(0, 0)
            pe.wait_ge(cnt_rdy, 1)
            te.matmul(ps_vk[:, 0:E], before[:], cnt[:], start=True, stop=True)
            te.matmul(ps_vk[:, 32:32 + E], ones[:], cnt[:], start=True, stop=True).then_inc(cnt_mm, 1)
            gate_up_shared(0, 3)
            down_shared(0, 1)

            def turn_y(c, first=False):
                pe.wait_ge(yT_sb, c + 1)
                pe.wait_ge(y_free, c + 1)
                for j in range(Q):
                    last = te.transpose(ps_y[:, P * j:P * j + P], yT[:, P * j:P * j + P], ident[:])
                last.then_inc(yT_mm, 1)

            def shared(lo, hi):
                if lo > 0:
                    for k in range(2, KC):
                        gate_up_shared(lo, k)
                        down_shared(lo, k - 2)
                with pe.Fori(lo + 1, hi) as c:
                    gate_up_shared(c, 0)
                    down_shared(c - 1, KC - 2)
                    gate_up_shared(c, 1)
                    down_shared(c - 1, KC - 1)
                    gate_up_shared(c, 2)
                    turn_y(c - 1)
                    down_shared(c, 0)
                    gate_up_shared(c, 3)
                    down_shared(c, 1)
                if hi < NQ:
                    experts(0, 0, (0,))
                down_shared(hi - 1, KC - 2)
                down_shared(hi - 1, KC - 1)
                turn_y(hi - 1)

            def columns(g, which):
                _, vals = nc.values_load_multi_w_load_instructions(
                    eid_flat[0:1, bass.ds((g * 2 + which) * Q, Q)], engines=(mybir.EngineType.PE,), min_val=0,
                    max_val=(E - 1) * D,
                    skip_runtime_bounds_check_because="VectorE made them as D * min(a count of experts, E - 1)")
                return vals

            eid_flat = eid[:].rearrange("o g s j -> o (g s j)")
            gu_cols = w_gu[:].rearrange("p s e c -> p s (e c)")
            dn_cols = w_dn[:].rearrange("p e c -> p (e c)")

            def experts(i, par, stages=(3, 2, 1, 0)):
                g = i * 2 + par
                if 0 in stages:
                    pe.wait_ge(xg_ld[par], (i + 1) * 16)
                    if not (isinstance(g, int) and g == 0):
                        pe.wait_ge(gT_sb, g)
                    for j in range(Q):
                        mm = te.transpose(ps_gT[:, P * j:P * j + P], xg[:, par, j, 0:D], ident[:])
                    mm.then_inc(gT_mm, 1)
                if 1 in stages:
                    cols = columns(g, 1)
                    pe.wait_ge(gT_sb, g)
                    for j in range(Q):
                        mm = split_product(gate_up_banks((par - 1) % 2)[:, j, :],
                                           xgT[:, (par - 1) % 2, :, P * j:P * j + P],
                                           gu_cols[:, :, bass.ds(cols[j] * 2, F2)])
                    mm.then_inc(e_gu_mm, 1)
                if 3 in stages:
                    cols = columns(g, 0)
                    pe.wait_ge(aT_sb, g - 2)
                    if not (isinstance(g, int) and g == 3):
                        pe.wait_ge(yg_rdy, g - 3)
                    for j in range(Q):
                        mm = te.matmul(ps_yg[:, P * j:P * j + P], e_actT[:, (par - 3) % 2, P * j:P * j + P],
                                       dn_cols[:, bass.ds(cols[j], D)], start=True, stop=True)
                    mm.then_inc(e_dn_mm, 1)
                if 2 in stages:
                    pe.wait_ge(e_act_rdy, g - 1)
                    if not (isinstance(g, int) and g == 2):
                        pe.wait_ge(aT_sb, g - 2)
                    for j in range(Q):
                        mm = te.transpose(ps_aT[:, P * j:P * j + P], e_act[:, par, j, :], ident[:])
                    mm.then_inc(aT_mm, 1)

            shared(0, C1)
            pe.wait_ge(eid_rdy, 2)
            pe.wait_ge(we_lo, E // EC)
            pe.wait_ge(ld_wd, 16)
            over_groups(experts, pe, lambda k: gate_up_shared(C1, k))
            shared(C1, NQ)


_INS = ["L0_attn_x", "L0_attn_Wq", "L0_attn_bq", "L0_attn_Wk", "L0_attn_bk", "L0_attn_Wv", "L0_attn_bv", "L0_attn_Wo",
        "L0_attn_bo", "L0_attn_m", "L0_ffn_router_w", "L0_ffn_gate_up_proj", "L0_ffn_down_proj",
        "L0_ffn_shared_gate_w", "L0_ffn_shared_up_w", "L0_ffn_shared_down_w"]


def kernel(**inputs):
    import concourse.bacc as bacc
    from concourse.bass_utils import run_bass_kernel_spmd

    nc = bacc.Bacc("TRN2", target_bir_lowering=False, num_devices=1)
    arrays = {name: np.ascontiguousarray(inputs[name]) for name in _INS}
    args = [nc.dram_tensor(name, a.shape, F32, kind="ExternalInput").ap() for name, a in arrays.items()]
    out = nc.dram_tensor("out", arrays["L0_attn_x"].shape, F32, kind="ExternalOutput").ap()
    build_block(nc, *args, out)
    return run_bass_kernel_spmd(nc, [arrays], core_ids=[0]).results[0]["out"]
```
